# Optimizing a Trainium2 kernel written in Bass

```python
import numpy as np
import jax
import jax.numpy as jnp

def _softmax(x, axis=-1):
    return jax.nn.softmax(x, axis=axis)

def _gelu(x):
    return jax.nn.gelu(x, approximate=True)

def _silu(x):
    return jax.nn.silu(x)

def _sigmoid(x):
    return jax.nn.sigmoid(x)

def _layernorm(x, axis=-1, eps=1e-05):
    m = jnp.mean(x, axis=axis, keepdims=True)
    v = jnp.var(x, axis=axis, keepdims=True)
    return (x - m) / jnp.sqrt(v + eps)

def _scatter_add(tgt, idx, src, axis=0):
    return tgt.at[idx].add(src)

def _segment_sum(src, seg, n):
    return jax.ops.segment_sum(src, seg, n)
kernel_name = 'mk_xattn_ffn_d1_seqx_r4_129f37'

def setup_inputs(seed: int=0):
    np.random.seed(seed)
    _w = jnp.asarray

    def _rec_inputs():
        import jax
        import jax.numpy as jnp
        _rk = jax.random.key(seed)
        x = 7.22e-05 + 1 * jax.random.normal(jax.random.fold_in(_rk, 1), (4, 512, 512), jnp.float32)
        _lenS = 512 - jax.random.randint(jax.random.fold_in(_rk, 7), (4,), 0, max(1, 512 // 4) + 1, jnp.int32)
        _lenS2 = 512 - jax.random.randint(jax.random.fold_in(_rk, 8), (4,), 0, max(1, 512 // 4) + 1, jnp.int32)
        _ctx_1024P = jax.random.normal(jax.random.fold_in(_rk, 11), (4, 16, 256), jnp.float32)
        _ctx_1024c = jax.random.dirichlet(jax.random.fold_in(_rk, 511), 0.3 * jnp.ones((16,), jnp.float32), (4, 512))
        _ctx_1024t = jnp.einsum('bsk,bkd->bsd', _ctx_1024c, _ctx_1024P)
        _ctx_1024t = _ctx_1024t * jax.lax.rsqrt(jnp.mean(jnp.square(_ctx_1024t)) + 1e-12) * 0.953939
        ctx_1024 = 2.81802e-05 + 1.00001 * (_ctx_1024t + 0.3 * jax.random.normal(jax.random.fold_in(_rk, 611), (4, 512, 256), jnp.float32))
        return (x, ctx_1024)
    x, ctx_1024 = _rec_inputs()

    def _L0_xattn_setup():
        import jax, jax.numpy as jnp
        import numpy as np
        key = jax.random.key(seed)
        ks = jax.random.split(key, 6)
        B, L, N, C, D = (8, 128, 512, 256, 128)
        return {'teacher_logits': jax.random.normal(ks[0], (B, L, N), dtype=jnp.float32), 'teacher_features': jax.random.normal(ks[1], (B, N, C), dtype=jnp.float32), 'Wq': jax.random.normal(ks[2], (D, C), dtype=jnp.float32) * (1.0 / np.sqrt(C)), 'bq': jnp.zeros((D,), dtype=jnp.float32), 'Wk': jax.random.normal(ks[3], (D, C), dtype=jnp.float32) * (1.0 / np.sqrt(C)), 'bk': jnp.zeros((D,), dtype=jnp.float32)}
    _L0_xattn_all = _L0_xattn_setup()
    _L0_xattn_in = {k: v for k, v in _L0_xattn_all.items() if k in ('Wq', 'bq', 'Wk', 'bk')}
    del _L0_xattn_all

    def _L0_ffn_setup():
        import jax, jax.numpy as jnp
        import numpy as np
        HIDDEN = 512
        INTER = 2048
        COMPRESSION = 128.9

        def _n_ctrl(out_size, in_size):
            return max(16, int(out_size * in_size / COMPRESSION))

        def _catmull_rom_grid(n_ctrl, n_samples):
            t = np.linspace(0.0, n_ctrl - 1.0, n_samples, dtype=np.float64)
            i = np.clip(np.floor(t).astype(np.int64), 0, n_ctrl - 2)
            f = (t - i).astype(np.float32)
            idx = np.stack([np.clip(i + k, 0, n_ctrl - 1) for k in (-1, 0, 1, 2)], axis=0)
            return (jnp.asarray(idx.astype(np.int32)), jnp.asarray(f))

        def spline_reconstruct(control_points, out_size, in_size):
            n = out_size * in_size
            idx, f = _catmull_rom_grid(control_points.shape[0], n)
            p0, p1, p2, p3 = (control_points[idx[0]], control_points[idx[1]], control_points[idx[2]], control_points[idx[3]])
            f2 = f * f
            f3 = f2 * f
            w = 0.5 * (2.0 * p1 + (p2 - p0) * f + (2.0 * p0 - 5.0 * p1 + 4.0 * p2 - p3) * f2 + (3.0 * p1 - p0 - 3.0 * p2 + p3) * f3)
            return w.reshape(out_size, in_size)
        key = jax.random.key(seed)
        k0, k1, k2, k3 = jax.random.split(key, 4)
        hidden_states = jax.random.normal(k0, (4, 512, HIDDEN), dtype=jnp.float32)
        gate_cp = jax.random.normal(k1, (_n_ctrl(INTER, HIDDEN),), dtype=jnp.float32) * 0.02
        up_cp = jax.random.normal(k2, (_n_ctrl(INTER, HIDDEN),), dtype=jnp.float32) * 0.02
        down_cp = jax.random.normal(k3, (_n_ctrl(HIDDEN, INTER),), dtype=jnp.float32) * 0.02
        return {'hidden_states': hidden_states, 'gate_cp': gate_cp, 'up_cp': up_cp, 'down_cp': down_cp}
    _L0_ffn_all = _L0_ffn_setup()
    _L0_ffn_in = {k: v for k, v in _L0_ffn_all.items() if k in ('gate_cp', 'up_cp', 'down_cp')}
    del _L0_ffn_all
    return {'x': x, 'ctx_1024': ctx_1024, 'L0_xattn_Wq': _L0_xattn_in['Wq'], 'L0_xattn_bq': _L0_xattn_in['bq'], 'L0_xattn_Wk': _L0_xattn_in['Wk'], 'L0_xattn_bk': _L0_xattn_in['bk'], 'L0_ffn_gate_cp': _L0_ffn_in['gate_cp'], 'L0_ffn_up_cp': _L0_ffn_in['up_cp'], 'L0_ffn_down_cp': _L0_ffn_in['down_cp']}

def reference(x, ctx_1024, L0_xattn_Wq, L0_xattn_bq, L0_xattn_Wk, L0_xattn_bk, L0_ffn_gate_cp, L0_ffn_up_cp, L0_ffn_down_cp):
    import jax
    import jax.numpy as jnp

    def _L0_xattn_ref(teacher_logits, teacher_features, Wq, bq, Wk, bk):
        import jax, jax.numpy as jnp
        import numpy as np
        query = jnp.einsum('bnc,dc->bnd', teacher_features, Wq) + bq
        key = jnp.einsum('bnc,dc->bnd', teacher_features, Wk) + bk
        energy = jnp.einsum('bnd,bmd->bnm', query, key)
        attention = jax.nn.softmax(energy, axis=-1)
        x_m = jnp.einsum('bln,bmn->blm', teacher_logits, attention)
        return x_m

    def _L0_ffn_ref(hidden_states, gate_cp, up_cp, down_cp):
        import jax, jax.numpy as jnp
        import numpy as np
        HIDDEN = 512
        INTER = 2048
        COMPRESSION = 128.9

        def _n_ctrl(out_size, in_size):
            return max(16, int(out_size * in_size / COMPRESSION))

        def _catmull_rom_grid(n_ctrl, n_samples):
            t = np.linspace(0.0, n_ctrl - 1.0, n_samples, dtype=np.float64)
            i = np.clip(np.floor(t).astype(np.int64), 0, n_ctrl - 2)
            f = (t - i).astype(np.float32)
            idx = np.stack([np.clip(i + k, 0, n_ctrl - 1) for k in (-1, 0, 1, 2)], axis=0)
            return (jnp.asarray(idx.astype(np.int32)), jnp.asarray(f))

        def spline_reconstruct(control_points, out_size, in_size):
            n = out_size * in_size
            idx, f = _catmull_rom_grid(control_points.shape[0], n)
            p0, p1, p2, p3 = (control_points[idx[0]], control_points[idx[1]], control_points[idx[2]], control_points[idx[3]])
            f2 = f * f
            f3 = f2 * f
            w = 0.5 * (2.0 * p1 + (p2 - p0) * f + (2.0 * p0 - 5.0 * p1 + 4.0 * p2 - p3) * f2 + (3.0 * p1 - p0 - 3.0 * p2 + p3) * f3)
            return w.reshape(out_size, in_size)
        gate_w = spline_reconstruct(gate_cp, INTER, HIDDEN)
        up_w = spline_reconstruct(up_cp, INTER, HIDDEN)
        down_w = spline_reconstruct(down_cp, HIDDEN, INTER)
        gate = jnp.einsum('bsh,ih->bsi', hidden_states, gate_w)
        up = jnp.einsum('bsh,ih->bsi', hidden_states, up_w)
        inter = jax.nn.silu(gate) * up
        return jnp.einsum('bsi,hi->bsh', inter, down_w)
    x = x + _L0_xattn_ref(_layernorm(x, axis=-1), ctx_1024, L0_xattn_Wq, L0_xattn_bq, L0_xattn_Wk, L0_xattn_bk)
    x = x + _L0_ffn_ref(_layernorm(x, axis=-1), L0_ffn_gate_cp, L0_ffn_up_cp, L0_ffn_down_cp)
    return x

_drawn_inputs = setup_inputs


def setup_inputs(seed=0):
    import zlib

    import numpy as np

    out = dict(_drawn_inputs(seed))
    spreads = {'L0_xattn_bq': (0.0, 0.1), 'L0_xattn_bk': (0.0, 0.1)}
    factors = {}
    for name, (base, spread) in spreads.items():
        noise = np.random.default_rng([zlib.crc32(name.encode()), seed]).standard_normal(out[name].shape)
        drawn = base * np.exp(spread * noise) if base else spread * noise
        out[name] = jnp.asarray(drawn.astype(out[name].dtype))
    for name, factor in factors.items():
        out[name] = (out[name] * factor).astype(out[name].dtype)
    return out
```

```python
import numpy as np
import concourse.bass as bass
from concourse import mybir
from contextlib import ExitStack

BF16 = mybir.dt.np(mybir.dt.bfloat16)
B, TOK, HID, CTX, DK, INTER = 4, 512, 512, 256, 128, 2048
NCTRL = int(INTER * HID / 128.9)
STEP = (NCTRL - 1) / (INTER * HID - 1)
PERIOD = 1 / STEP
P = 128
NT = HID // P
CLS = 4
MT = INTER // P
G_NODES = 4 * CLS + 1
G_FN = 2 * G_NODES
G_K = 3 * G_FN
WIN = 4
D_NODES = 16
D_FN = 2 * D_NODES
D_CELLS = WIN * (D_NODES - 1)
WIDTH = PERIOD / 4
S2, S3 = 256.0, 2048.0
EPS = 1e-5


def hermite(u):
    return 2 * u**3 - 3 * u**2 + 1, u**3 - 2 * u**2 + u, 3 * u**2 - 2 * u**3, u**3 - u**2


def basis_at(pos, nodes):
    c = np.clip(np.searchsorted(nodes, pos, side="right") - 1, 0, len(nodes) - 2)
    width = nodes[c + 1] - nodes[c]
    out = np.zeros((len(pos), 2 * len(nodes)))
    for k, h in enumerate(hermite((pos - nodes[c]) / width)):
        out[np.arange(len(pos)), 2 * c + k] = h * (width / WIDTH if k % 2 else 1)
    return out, c


def node_taps(t):
    k = np.floor(t).astype(np.int64)
    f = t - k
    value = 0.5 * np.stack([-f + 2 * f**2 - f**3, 2 - 5 * f**2 + 3 * f**3, f + 4 * f**2 - 3 * f**3, f**3 - f**2], -1)
    slope = 0.5 * np.stack([4 * f - 1 - 3 * f**2, 9 * f**2 - 10 * f, 1 + 8 * f - 9 * f**2, 3 * f**2 - 2 * f], -1)
    return control(k[..., None] + np.arange(-1, 3)), np.stack([value, slope * (WIDTH * STEP)], -2)


def control(k):
    return np.clip(k, 0, NCTRL - 1)


def cell_residual(pos, left, right, knot):
    inside = (knot > left) & (knot < right)
    knot = np.where(inside, knot, right)
    width = right - left
    _, _, value, slope = hermite((pos - left) / width)
    x, e = np.maximum(pos - knot, 0) * STEP, (right - knot) * STEP
    r2 = x**2 - (value * e**2 + slope * 2 * e * width * STEP)
    r3 = x**3 - (value * e**3 + slope * 3 * e**2 * width * STEP)
    return np.where(inside, r2, 0) * S2, np.where(inside, r3, 0) * S3


def gate_layout():
    start = np.arange(INTER) * HID * STEP
    first = PERIOD * (1 - (start - np.floor(start)))
    for offset in np.arange(-4.7, 0, 0.1):
        turn = (first - offset) % PERIOD
        order = np.sort(turn)
        edge = np.array([0] + [order[a * HID - 1:a * HID + 1].mean() for a in range(1, CLS)])
        nodes = np.append((offset + np.arange(4)[:, None] * PERIOD + edge).ravel(), offset + 4 * PERIOD)
        cell = np.searchsorted(nodes, np.arange(HID), side="right") - 1
        if nodes[-1] >= HID - 1 and (np.bincount(cell % CLS) == P).all():
            break
    else:
        raise ValueError("no layout with equal classes")
    cls = np.searchsorted(edge, turn, side="right") - 1
    hidden = np.argsort(cell % CLS, kind="stable")
    rows = np.stack([np.flatnonzero(cls == a) for a in range(CLS)]).reshape(CLS, WIN, P)
    knot = np.rint(start + (offset + turn) * STEP).astype(np.int64)
    return nodes, cell, hidden, rows, knot, start


def constants():
    nodes, cell, hidden, rows, knot, start = gate_layout()
    c, at = {}, {}
    tiles = rows.transpose(1, 0, 2).reshape(MT, P)
    idx, coef = node_taps(start[tiles.T][:, :, None] + nodes * STEP)
    at["g_node"] = idx.reshape(P, MT * G_NODES, 4)
    c["g_coef"] = coef.reshape(P, MT * G_NODES * 8).astype(np.float32)
    u = basis_at(hidden.astype(float), nodes)[0].reshape(CLS, P, G_FN)
    c["g_basis"] = np.tile(u.transpose(1, 0, 2)[:, :, None], (1, 1, 3, 1)).reshape(P, CLS * G_K).astype(np.float32)
    lo = (np.arange(G_K) // G_FN) == 1
    c["g_low"] = np.where(lo, -1.0, 0.0).reshape(G_K, 1).astype(np.float32)
    byclass = rows.reshape(INTER)
    at["g_win"] = control(knot[byclass] + np.arange(-2, 6)[:, None])
    jump = {2: np.array([0.5, -1, 0, 1, -0.5]), 3: np.array([0.5, -2, 3, -2, 0.5])}
    pick = np.zeros((8, CLS, 2, P))
    r2, r3 = np.zeros((P, INTER)), np.zeros((P, INTER))
    for a in range(CLS):
        h = hidden[a * P:(a + 1) * P]
        for n in range(4):
            pick[n:n + 5, a, 0, cell[h] // CLS == n] = jump[2][:, None] / S2
            pick[n:n + 5, a, 1, cell[h] // CLS == n] = jump[3][:, None] / S3
        i = rows[a].ravel()
        place = ((knot[i] + (cell[h] // CLS)[:, None]) - start[i]) * PERIOD
        left, right = nodes[cell[h]][:, None], nodes[cell[h] + 1][:, None]
        r2[:, a * HID:(a + 1) * HID], r3[:, a * HID:(a + 1) * HID] = cell_residual(h[:, None], left, right, place)
    c["g_pick"] = pick.reshape(8, CLS * 2 * P).astype(BF16)
    c["g_r2"], c["g_r3"] = r2.astype(np.float16), r3.astype(np.float16)
    window = tiles.reshape(WIN, CLS * P)
    dn = np.stack([np.linspace(w.min(), w.max(), D_NODES) for w in window])
    t = hidden.reshape(NT, P).T[:, :, None] * (INTER * STEP) + dn.ravel() * STEP
    idx, coef = node_taps(t)
    at["d_node"] = idx.reshape(P, NT * WIN * D_NODES, 4)
    c["d_coef"] = coef.reshape(P, NT * WIN * D_NODES * 8).astype(np.float32)
    basis, spread = np.zeros((P, MT, D_FN)), np.zeros((D_CELLS, MT, P))
    left, right = dn[:, :-1].ravel(), dn[:, 1:].ravel()
    row0 = hidden * (INTER * STEP)
    kd = np.floor(row0 + right[:, None] * STEP).astype(np.int64)
    at["d_knot"] = control(kd[:, None] + np.arange(-2, 3)[:, None])
    place = (kd - row0) * PERIOD
    r2, r3 = np.zeros((P, MT, HID)), np.zeros((P, MT, HID))
    for m in range(MT):
        basis[:, m], k = basis_at(tiles[m].astype(float), dn[m // CLS])
        k = k + (m // CLS) * (D_NODES - 1)
        spread[k, m, np.arange(P)] = 1
        r2[:, m], r3[:, m] = cell_residual(tiles[m][:, None], left[k][:, None], right[k][:, None], place[k])
    c["d_basis"] = basis.reshape(P, MT * D_FN).astype(np.float32)
    c["d_spread"] = spread.reshape(D_CELLS, INTER).astype(BF16)
    c["d_r2"], c["d_r3"] = (r.reshape(P, 4, 4 * HID).transpose(1, 0, 2).astype(np.float16) for r in (r2, r3))
    c["d_low"] = np.where(np.arange(P) // D_FN == 1, -1.0, 0.0).reshape(P, 1).astype(np.float32)
    c["ident"] = np.eye(P, dtype=np.float32)
    return c, at, hidden, tiles


def xattn_spline_ffn_kernel(nc: bass.Bass, d, out: bass.AP):
    f32, f32r, bf16, fp16 = mybir.dt.float32, mybir.dt.float32r, mybir.dt.bfloat16, mybir.dt.float16
    ALU, ACT, AX = mybir.AluOpType, mybir.ActivationFunctionType, mybir.AxisListType

    ctx = ExitStack()
    with ctx:
        def sb(name, shape, dt, stack=ctx):
            return stack.enter_context(nc.sbuf_tensor(name, shape, dt))

        def sem(name):
            return ctx.enter_context(nc.semaphore(name))

        wqk = sb("wqk", [P, 2, CTX // P, DK], f32)
        bqk = sb("bqk", [DK, 2], f32)
        ident = sb("ident", [P, P], f32)
        g_basis = sb("g_basis", [P, CLS, G_K], f32)
        g_low = sb("g_low", [G_K, 1], f32)
        d_low = sb("d_low", [P, 1], f32)
        neghalf = sb("neghalf", [P, NT], f32)
        eps = sb("eps", [P, NT], f32)
        ones = sb("ones", [P, 1, 1], f32)
        gu_r = [sb(f"{n}_r", [P, CLS, WIN * P], f32r) for n in ("gate", "up")]
        gu_v = [sb(f"{n}_v", [G_K, MT, P], f32r) for n in ("gate", "up")]
        d_v = sb("d_v", [P, WIN, HID], f32r)
        d_u = sb("d_u", [P, MT, 4, D_FN], f32r)
        ctxT = sb("ctxT", [P, CTX // P, TOK], f32)
        qk = sb("qk", [P, 2, TOK], f32)
        x = sb("x", [P, NT, HID], f32)
        xT = sb("xT", [P, NT, TOK], f32)
        xh = sb("xh", [P, NT, TOK], f32r)
        xl = sb("xl", [P, NT, TOK], f32r)
        prob = sb("prob", [P, NT, TOK], f32)
        ph = sb("ph", [P, NT, TOK], f32r)
        pl = sb("pl", [P, NT, TOK], f32r)
        nmax = sb("nmax", [P, NT], f32)
        rsum = sb("rsum", [P, NT], f32)
        rinv = sb("rinv", [P, NT], f32)
        bst1, bst2 = sb("bst1", [P, NT, 6], f32), sb("bst2", [P, NT, 6], f32)
        mv1, mv2 = sb("mv1", [P, NT, 2], f32), sb("mv2", [P, NT, 2], f32)
        ve1, ve2 = sb("ve1", [P, NT], f32), sb("ve2", [P, NT], f32)
        rstd1, rstd2 = sb("rstd1", [P, NT], f32), sb("rstd2", [P, NT], f32)
        nmr1 = sb("nmr1", [P, NT], f32)
        xn2, xn2T, xn2r, xm = xT, prob, xh, qk

        prep = ExitStack()
        coef = sb("coef", [P, MT * G_NODES * 8], f32, prep)
        taps = [sb(f"taps{n}", [P, MT * G_NODES * 4], f32, prep) for n in range(2)]
        prod = sb("prod", [P, MT * G_NODES * 8], f32, prep)
        fval = sb("fval", [P, MT * G_FN], f32, prep)
        sb("pad", [P, (32768 - 4 * (MT * G_NODES * (8 + 4 + 4 + 8) + MT * G_FN)) // 4], f32, prep)
        stack = sb("stack", [P, 2048], f32, prep)
        prod2 = sb("prod2", [P, 2, 2, HID], f32, prep)
        work = sb("work", [P, 6656], f32, prep)
        knots = sb("knots", [D_CELLS, 5, HID], f32, prep)
        spread = sb("spread", [D_CELLS, MT, P], bf16, prep)
        prep.close()
        d_r = sb("d_r", [P, MT, HID], f32r)
        ih = sb("ih", [P, MT, TOK], f32r)
        xres = sb("xres", [P, NT, HID], f32)
        high = sb("high", [P, TOK], f32)
        inter = sb("inter", [P, 2, TOK], f32)
        il = sb("il", [P, 2, TOK], f32r)
        zd = sb("zd", [P, WIN, TOK], f32r)
        zg = zd[0:G_K, WIN - 1, :]

        r2g, r3g = (work[:, n * 1024:(n + 1) * 1024].bitcast(fp16) for n in range(2))
        win = work[0:40, 2048:4096]
        win_h, win_l = (work[0:40, 4096 + n * 1024:5120 + n * 1024].bitcast(bf16) for n in range(2))
        pick = work[0:40, 6144:6656].bitcast(bf16).rearrange("p (a k n) -> p a k n", a=CLS, k=2)
        rd = [[work[:, s * 2048 + n * 1024:s * 2048 + (n + 1) * 1024].bitcast(fp16) for n in range(2)] for s in range(3)]
        ja, jb = (stack[0:D_CELLS, n * 512:(n + 1) * 512] for n in range(2))
        jump = [[stack[0:D_CELLS, 1024 + n * 256:1280 + n * 256].bitcast(bf16) for n in (2 * k, 2 * k + 1)] for k in range(2)]

        bank = [ctx.enter_context(nc.psum_tensor(f"bank{n}", [P, 512], f32)) for n in range(8)]
        gbank, ubank, obank = bank[0:2], bank[2:4], bank[0:4]
        zgbank, zdbank = bank[4], [bank[5], bank[4], bank[5], bank[4]]
        abank = bank[6:8]

        names = """w_in ctx_in x_in xt_in win_in r_in node_in coefg_in upnode_in coefd_in dnode_in dbasis_in knot_in
            rd0_in rd1_in rd2_in out_stored
            consts_set win_hi win_split jump_a jump_b jump_d jump_hi jump_split res_mm res_mul res_done
            tap_mul tap_sum stack_hi stack_done stack_mm stack_out du_hi du_done
            qk_mm qk_done energy_mm max_done exp_done rinv_done prob_done pT_mm ph_done pl_done
            stats1 mv1_done ve1_done rstd1_done nmr_done xh_done xsplit_done xm_mm xm_scaled x1_added
            stats2 mv2_done ve2_done rstd2_done xn2_done xn2T_mm xn2t_copied xn2r_done
            x1_kept zg_mm zg_hi zg_done g_mm u_mm silu_done mult_done ih_done il_done zd_mm zd_hi zd_done
            out_mm out_added"""
        s = {n: sem(n) for n in names.split()}

        def attention_only(st):
            st.split_windows()
            st.qk(0)
            st.stats(0)
            for t in range(NT):
                st.energy(0, t)
            for t in range(NT):
                st.scale(0, t)
            for r in range(2 * CLS):
                st.residual(r)
            for t in range(NT):
                st.prob_t(0, t)
            st.split_x(0)
            for n in range(2):
                st.coefficients(n)
            for t in range(NT):
                st.xm(0, t)
            st.coefficients(2)
            st.jumps()
            for r in range(2 * CLS, 2 * CLS + MT):
                st.residual(r)
            for t in range(NT):
                st.norm_t(0, t)

        def ffn(st, b, a=None):
            st.project(b)
            for m in range(MT):
                st.gate_up(b, m)
                if m >= 2:
                    st.down_basis(b, m - 2)
                    if m % CLS == 1:
                        st.down_split(b, m // CLS - 1)
                if a is not None:
                    if m == 1:
                        st.qk(a)
                    if m == 3:
                        st.energy(a, 0)
                        st.energy(a, 1)
                    if m == 4:
                        st.energy(a, 2)
                        st.energy(a, 3)
                    if m == 6:
                        for t in range(NT):
                            st.scale(a, t)
                    if m == 7:
                        st.stats(a)
                    if 9 <= m < 9 + NT:
                        st.prob_t(a, m - 9)
            st.down_basis(b, MT - 2)
            st.down_basis(b, MT - 1)
            st.down_split(b, WIN - 1)
            if a is not None:
                st.split_x(a)
            st.down(b, 0)
            if a is not None:
                for t in range(NT):
                    st.xm(a, t)
            st.down(b, 1)
            st.down(b, 2)
            if a is not None:
                for t in range(NT):
                    st.norm_t(a, t)
            st.down(b, 3)

        def program(eng, st):
            attention_only(st)
            with eng.Fori(0, B - 1) as b:
                ffn(st, b, b + 1)
            ffn(st, B - 1)

        block = ctx.enter_context(nc.Block())

        @block.sync
        def _(sp):
            def load(dst, name, signal):
                sp.dma_start(dst, d[name]).then_inc(s[signal], 16)

            load(wqk[:, 0], "wqT", "w_in")
            load(wqk[:, 1], "wkT", "w_in")
            load(bqk[:, 0:1], "bq", "w_in")
            load(bqk[:, 1:2], "bk", "w_in")
            load(ident[:], "ident", "w_in")
            sp.dma_start(ctxT[:], d["ctxT"][0]).then_inc(s["ctx_in"], 16)
            for n, name in enumerate(("g_win", "u_win")):
                load(win[32 * n:32 * n + 8, :], name, "win_in")
                load(work[32 * n:32 * n + 8, 6144:6656].bitcast(bf16), "g_pick", "win_in")
            load(r2g, "g_r2", "r_in")
            load(r3g, "g_r3", "r_in")
            sp.dma_start(x[:], d["x"][0]).then_inc(s["x_in"], 16)
            sp.dma_start(xT[:], d["xT"][0]).then_inc(s["xt_in"], 16)
            load(coef[:], "g_coef", "coefg_in")
            load(taps[0][:], "g_node", "node_in")
            load(taps[1][:], "u_node", "upnode_in")
            load(g_basis[:].rearrange("p a n -> p (a n)"), "g_basis", "w_in")
            load(g_low[:], "g_low", "w_in")
            load(d_low[:], "d_low", "w_in")
            load(knots[:].rearrange("p w n -> p (w n)"), "d_knot", "knot_in")
            load(spread[:].rearrange("p m n -> p (m n)"), "d_spread", "knot_in")
            sp.wait_ge(s["res_mul"], 16)
            for n in range(2):
                sp.dma_start(rd[0][n], d[f"d_r{n + 2}"][0]).then_inc(s["rd0_in"], 16)
                sp.dma_start(rd[1][n], d[f"d_r{n + 2}"][1]).then_inc(s["rd1_in"], 16)
                sp.dma_start(rd[2][n], d[f"d_r{n + 2}"][2]).then_inc(s["rd2_in"], 16)
            sp.wait_ge(s["tap_mul"], 2)
            load(coef[:, 0:NT * WIN * D_NODES * 8], "d_coef", "coefd_in")
            load(taps[0][:, 0:NT * WIN * D_NODES * 4], "d_node", "dnode_in")
            load(taps[1][:, 0:MT * D_FN], "d_basis", "dbasis_in")
            sp.wait_ge(s["res_mul"], 2 * (2 * CLS + 4))
            for n in range(2):
                sp.dma_start(rd[0][n], d[f"d_r{n + 2}"][3]).then_inc(s["rd0_in"], 16)

            def store(b, t):
                sp.wait_ge(s["out_added"], NT * b + t + 1)
                sp.dma_start(out[bass.ds(b, 1), t].rearrange("a p n -> (a p) n"), xres[:, t]).then_inc(s["out_stored"], 16)

            def fetch(src, b):
                return d[src][bass.ds(b, 1)].rearrange("a p t n -> (a p) t n")

            with sp.Fori(0, B - 1) as b:
                if True:
                    sp.wait_ge(s["qk_mm"], 2 * b + 2)
                    sp.dma_start(ctxT[:], fetch("ctxT", b + 1)).then_inc(s["ctx_in"], 16)
                    sp.wait_ge(s["xn2_done"], NT * (b + 1))
                    sp.wait_ge(s["x1_kept"], b + 1)
                    sp.dma_start(x[:], fetch("x", b + 1)).then_inc(s["x_in"], 16)
                    sp.wait_ge(s["xn2T_mm"], NT * (b + 1))
                    sp.dma_start(xT[:], fetch("xT", b + 1)).then_inc(s["xt_in"], 16)
                for t in range(NT):
                    store(b, t)
            for t in range(NT):
                store(B - 1, t)
            sp.wait_ge(s["out_stored"], 16 * NT * B)

        @block.scalar
        def _(act):
            class Stages:
                def split_windows():
                    act.wait_ge(s["win_in"], 64)
                    for p in (0, 32):
                        nc.scalar.activation(win_h[p:p + 8], win[p:p + 8], ACT.Copy).then_inc(s["win_hi"], 1)

                def qk(b):
                    for n in range(2):
                        act.wait_ge(s["qk_mm"], 2 * b + n + 1)
                        if n == 0:
                            act.wait_ge(s["w_in"], 8 * 16)
                            if not (isinstance(b, int) and b == 0):
                                act.wait_ge(s["x1_added"], NT * b)
                        nc.scalar.activation(qk_[:, n], abank[n][:], ACT.Identity, bias=bqk[:, n:n + 1]).then_inc(s["qk_done"], 1)

                def stats(b):
                    pass

                def energy(b, t):
                    act.wait_ge(s["max_done"], NT * b + t + 1)
                    if t == 0 and not (isinstance(b, int) and b == 0):
                        act.wait_ge(s["zg_mm"], b)
                    nc.scalar.activation(prob[:, t], abank[t % 2][:], ACT.Exp, bias=nmax[:, t:t + 1],
                                         accum_out=rsum[:, t:t + 1]).then_inc(s["exp_done"], 1)

                def scale(b, t):
                    pass

                def residual(r):
                    pass

                def prob_t(b, t):
                    act.wait_ge(s["pT_mm"], NT * b + t + 1)
                    nc.scalar.activation(ph[:, t], abank[t % 2][:], ACT.Copy).then_inc(s["ph_done"], 1)

                def split_x(b):
                    pass

                def coefficients(n):
                    act.wait_ge(s["tap_sum"], n + 1)
                    if n:
                        act.wait_ge(s["stack_mm"], 4 * n)
                    if n < 2:
                        st3 = stack[:, 0:MT * G_K].bitcast(f32r).rearrange("p (m k f) -> p m k f", m=MT, k=3)
                        v = fval[:].rearrange("p (m f) -> p m f", m=MT)
                        slots = (0, 1)
                    else:
                        st3 = stack[:].bitcast(f32r).rearrange("p (m k f) -> p m k f", m=NT * WIN, k=4)
                        v = fval[:, 0:NT * WIN * D_FN].rearrange("p (m f) -> p m f", f=D_FN)
                        slots = (0, 1, 2)
                    for k in slots:
                        last = nc.scalar.activation(st3[:, :, k], v, ACT.Copy)
                    last.then_inc(s["stack_hi"], 1)
                    for g in range(4):
                        act.wait_ge(s["stack_mm"], 4 * n + g + 1)
                        if n < 2:
                            dst = gu_v[n][:, 4 * g:4 * g + 4].rearrange("p m i -> p (m i)")
                        else:
                            dst = d_v[:, g]
                        nc.scalar.activation(dst, bank[4 + g % 2][0:dst.shape[0], :], ACT.Copy).then_inc(s["stack_out"], 1)
                    if n == 2:
                        act.wait_ge(s["dbasis_in"], 16)
                        u = taps[1][:, 0:MT * D_FN].rearrange("p (m f) -> p m f", m=MT)
                        for k in (0, 1, 3):
                            last = nc.scalar.activation(d_u[:, :, k], u, ACT.Copy)
                        last.then_inc(s["du_hi"], 1)

                def jumps():
                    for k in range(2):
                        act.wait_ge(s["jump_d"], k + 1)
                        nc.scalar.activation(jump[k][0], ja, ACT.Copy).then_inc(s["jump_hi"], 1)

                def xm(b, t):
                    act.wait_ge(s["xm_mm"], NT * b + t + 1)
                    if t == 0:
                        act.wait_ge(s["nmr_done"], b + 1)
                    if t >= 2:
                        act.wait_ge(s["x1_added"], NT * b + t - 1)
                    nc.scalar.activation(xm_[:, t % 2], abank[t % 2][:], ACT.Identity, bias=nmr1[:, t:t + 1],
                                         scale=rstd1[:, t:t + 1]).then_inc(s["xm_scaled"], 1)

                def norm_t(b, t):
                    act.wait_ge(s["xn2T_mm"], NT * b + t + 1)
                    nc.scalar.activation(xn2T[:, t], abank[t % 2][:], ACT.Copy).then_inc(s["xn2t_copied"], 1)

                def project(b):
                    act.wait_ge(s["zg_mm"], b + 1)
                    if isinstance(b, int) and b == 0 or not isinstance(b, int):
                        act.wait_ge(s["res_done"], 2 * CLS + MT)
                    act.wait_ge(s["zd_done"], WIN * b)
                    nc.scalar.activation(high[0:G_K].bitcast(f32r), zgbank[0:G_K, :], ACT.Copy).then_inc(s["zg_hi"], 1)

                def gate_up(b, m):
                    act.wait_ge(s["g_mm"], MT * b + m + 1)
                    if m >= 2:
                        act.wait_ge(s["il_done"], MT * b + m - 1)
                    nc.scalar.activation(inter[:, m % 2], gbank[m % 2][:], ACT.Silu).then_inc(s["silu_done"], 1)

                def down_basis(b, m):
                    pass

                def down_split(b, w):
                    act.wait_ge(s["zd_mm"], MT * b + CLS * (w + 1))
                    if w == 0:
                        act.wait_ge(s["zg_done"], b + 1)
                    else:
                        act.wait_ge(s["zd_done"], WIN * b + w)
                    nc.scalar.activation(high[:].bitcast(f32r), zdbank[w][:], ACT.Copy).then_inc(s["zd_hi"], 1)

                def down(b, t):
                    pass

            qk_, xm_ = qk, xm
            program(act, Stages)

        @block.vector
        def _(dve):
            V = nc.vector

            class Stages:
                def split_windows():
                    V.memset(eps[:], EPS)
                    V.memset(ones[:], 1.0)
                    V.memset(neghalf[:], -0.5).then_inc(s["consts_set"], 1)
                    for n, p in enumerate((0, 32)):
                        dve.wait_ge(s["win_hi"], n + 1)
                        V.tensor_tensor(win_l[p:p + 8], win[p:p + 8], win_h[p:p + 8], ALU.subtract).then_inc(s["win_split"], 1)

                def qk(b):
                    pass

                def stats(b):
                    dve.wait_ge(s["x_in"], 16 * (b + 1))
                    for t in range(NT):
                        last = V.bn_stats(bst1[:, t], x[:, t])
                    last.then_inc(s["stats1"], 1)
                    dve.wait_ge(s["consts_set"], 1)
                    dve.wait_ge(s["stats1"], b + 1)
                    for t in range(NT):
                        last = V.bn_aggr(mv1[:, t], bst1[:, t])
                    last.then_inc(s["mv1_done"], 1)
                    dve.wait_ge(s["rstd1_done"], b + 1)
                    V.scalar_tensor_tensor(nmr1[:], mv1[:, :, 0], -1.0, rstd1[:], ALU.mult, ALU.mult).then_inc(s["nmr_done"], 1)

                def energy(b, t):
                    dve.wait_ge(s["energy_mm"], NT * b + t + 1)
                    V.tensor_reduce(nmax[:, t:t + 1], abank[t % 2][:], AX.X, ALU.max, negate=True).then_inc(s["max_done"], 1)

                def scale(b, t):
                    dve.wait_ge(s["exp_done"], NT * b + t + 1)
                    V.reciprocal(rinv[:, t:t + 1], rsum[:, t:t + 1]).then_inc(s["rinv_done"], 1)
                    dve.wait_ge(s["rinv_done"], NT * b + t + 1)
                    V.tensor_scalar(prob[:, t], prob[:, t], rinv[:, t:t + 1], None, ALU.mult).then_inc(s["prob_done"], 1)

                def residual(r):
                    dve.wait_ge(s["res_mm"], r + 1)
                    if r == 0:
                        dve.wait_ge(s["r_in"], 32)
                    if r >= 2:
                        dve.wait_ge(s["res_done"], r - 1)
                    if r < 2 * CLS:
                        c = slice(r % CLS * HID, (r % CLS + 1) * HID)
                        parts = r2g[:, c], r3g[:, c]
                    else:
                        m = r - 2 * CLS
                        if m % 4 == 0:
                            dve.wait_ge(s[f"rd{m // 4 % 3}_in"], 32 * (m // 12 + 1))
                        parts = (rd[m // 4 % 3][n][:, m % 4 * HID:(m % 4 + 1) * HID] for n in range(2))
                    for k, part in enumerate(parts):
                        V.tensor_tensor(prod2[:, r % 2, k], bank[2 * (r % 2) + k][:], part, ALU.mult).then_inc(s["res_mul"], 1)

                def prob_t(b, t):
                    dve.wait_ge(s["ph_done"], NT * b + t + 1)
                    V.tensor_tensor(pl[:, t], abank[t % 2][:], ph[:, t].bitcast(f32), ALU.subtract).then_inc(s["pl_done"], 1)

                def split_x(b):
                    dve.wait_ge(s["xt_in"], 16 * (b + 1))
                    dve.wait_ge(s["u_mm"], MT * b)
                    V.tensor_copy(xh[:], xT[:]).then_inc(s["xh_done"], 1)
                    dve.wait_ge(s["xh_done"], b + 1)
                    V.tensor_tensor(xl[:], xT[:], xh[:].bitcast(f32), ALU.subtract).then_inc(s["xsplit_done"], 1)

                def coefficients(n):
                    for need, count in ((("coefg_in", 16), ("node_in", 16)), (("upnode_in", 16),),
                                        (("coefd_in", 16), ("dnode_in", 16)))[n]:
                        dve.wait_ge(s[need], count)
                    nodes = MT * G_NODES if n < 2 else NT * WIN * D_NODES
                    if n:
                        dve.wait_ge(s["stack_hi"], n)
                    c = coef[:, 0:nodes * 8].rearrange("p (n v t) -> p n v t", v=2, t=4)
                    tp = taps[n % 2][:, 0:nodes * 4].rearrange("p (n a t) -> p n a t", a=1, t=4).broadcast_to([P, nodes, 2, 4])
                    pr = prod[:, 0:nodes * 8]
                    V.tensor_tensor(pr.rearrange("p (n v t) -> p n v t", v=2, t=4), c, tp, ALU.mult).then_inc(s["tap_mul"], 1)
                    dve.wait_ge(s["tap_mul"], n + 1)
                    V.tensor_reduce(fval[:, 0:nodes * 2], pr.rearrange("p (n t) -> p n t", t=4), AX.X, ALU.add).then_inc(s["tap_sum"], 1)
                    dve.wait_ge(s["stack_hi"], n + 1)
                    if n < 2:
                        st3 = stack[:, 0:MT * G_K].rearrange("p (m k f) -> p m k f", m=MT, k=3)
                        v, lo = fval[:].rearrange("p (m f) -> p m f", m=MT), 2
                    else:
                        st3 = stack[:].rearrange("p (m k f) -> p m k f", m=NT * WIN, k=4)
                        v, lo = fval[:, 0:NT * WIN * D_FN].rearrange("p (m f) -> p m f", f=D_FN), 3
                    V.tensor_tensor(st3[:, :, lo].bitcast(f32r), v, st3[:, :, 0], ALU.subtract).then_inc(s["stack_done"], 1)
                    if n == 2:
                        dve.wait_ge(s["du_hi"], 1)
                        u = taps[1][:, 0:MT * D_FN].rearrange("p (m f) -> p m f", m=MT)
                        V.tensor_tensor(d_u[:, :, 2], u, d_u[:, :, 0].bitcast(f32), ALU.subtract).then_inc(s["du_done"], 1)

                def jumps():
                    dve.wait_ge(s["knot_in"], 32)
                    dve.wait_ge(s["stack_mm"], 12)
                    k0, k1, k2, k3, k4 = (knots[:, w] for w in range(5))
                    V.tensor_tensor(ja, k0, k4, ALU.subtract)
                    V.tensor_tensor(jb, k1, k3, ALU.subtract).then_inc(s["jump_a"], 1)
                    dve.wait_ge(s["jump_a"], 1)
                    V.tensor_scalar(ja, ja, 0.5 / S2, None, ALU.mult).then_inc(s["jump_b"], 1)
                    dve.wait_ge(s["jump_b"], 1)
                    V.scalar_tensor_tensor(ja, jb, -1 / S2, ja, ALU.mult, ALU.add).then_inc(s["jump_d"], 1)
                    dve.wait_ge(s["jump_hi"], 1)
                    V.tensor_tensor(jump[0][1], ja, jump[0][0], ALU.subtract).then_inc(s["jump_split"], 1)
                    dve.wait_ge(s["jump_split"], 1)
                    V.tensor_tensor(ja, k0, k4, ALU.add)
                    V.tensor_tensor(jb, k1, k3, ALU.add).then_inc(s["jump_a"], 1)
                    dve.wait_ge(s["jump_a"], 2)
                    V.tensor_scalar(ja, ja, 0.5 / S3, None, ALU.mult).then_inc(s["jump_b"], 1)
                    dve.wait_ge(s["jump_b"], 2)
                    V.scalar_tensor_tensor(ja, jb, -2 / S3, ja, ALU.mult, ALU.add).then_inc(s["jump_b"], 1)
                    dve.wait_ge(s["jump_b"], 3)
                    V.scalar_tensor_tensor(ja, k2, 3 / S3, ja, ALU.mult, ALU.add).then_inc(s["jump_d"], 1)
                    dve.wait_ge(s["jump_hi"], 2)
                    V.tensor_tensor(jump[1][1], ja, jump[1][0], ALU.subtract).then_inc(s["jump_split"], 1)

                def xm(b, t):
                    dve.wait_ge(s["xm_scaled"], NT * b + t + 1)
                    V.tensor_tensor(x[:, t], x[:, t], xm_[:, t % 2], ALU.add).then_inc(s["x1_added"], 1)
                    dve.wait_ge(s["x1_added"], NT * b + t + 1)
                    V.bn_stats(bst2[:, t], x[:, t]).then_inc(s["stats2"], 1)
                    dve.wait_ge(s["consts_set"], 1)
                    dve.wait_ge(s["stats2"], NT * b + t + 1)
                    V.bn_aggr(mv2[:, t], bst2[:, t]).then_inc(s["mv2_done"], 1)
                    if t:
                        normalise(b, t - 1)
                    if t == NT - 1:
                        normalise(b, t)

                def norm_t(b, t):
                    dve.wait_ge(s["xn2t_copied"], NT * b + t + 1)
                    V.tensor_copy(xn2r[:, t], xn2T[:, t]).then_inc(s["xn2r_done"], 1)

                def project(b):
                    dve.wait_ge(s["zg_hi"], b + 1)
                    dve.wait_ge(s["out_mm"], NT * b)
                    dve.wait_ge(s["w_in"], 8 * 16)
                    V.scalar_tensor_tensor(zg, high[0:G_K], g_low[:], zgbank[0:G_K, :], ALU.mult, ALU.add).then_inc(s["zg_done"], 1)

                def gate_up(b, m):
                    dve.wait_ge(s["silu_done"], MT * b + m + 1)
                    dve.wait_ge(s["u_mm"], MT * b + m + 1)
                    V.tensor_tensor(inter[:, m % 2], inter[:, m % 2], ubank[m % 2][:], ALU.mult).then_inc(s["mult_done"], 1)
                    dve.wait_ge(s["mult_done"], MT * b + m + 1)
                    V.tensor_copy(ih[:, m], inter[:, m % 2]).then_inc(s["ih_done"], 1)

                def down_basis(b, m):
                    pass

                def down_split(b, w):
                    dve.wait_ge(s["zd_hi"], WIN * b + w + 1)
                    V.scalar_tensor_tensor(zd[:, w], high[:], d_low[:], zdbank[w][:], ALU.mult, ALU.add).then_inc(s["zd_done"], 1)

                def down(b, t):
                    dve.wait_ge(s["out_mm"], NT * b + t + 1)
                    dve.wait_ge(s["x1_kept"], b + 1)
                    V.tensor_tensor(xres[:, t], xres[:, t], obank[t][:], ALU.add).then_inc(s["out_added"], 1)

            def normalise(b, t):
                dve.wait_ge(s["rstd2_done"], NT * b + t + 1)
                V.tensor_scalar(xn2[:, t], x[:, t], mv2[:, t, 0:1], rstd2[:, t:t + 1], ALU.subtract, ALU.mult).then_inc(s["xn2_done"], 1)

            xm_ = xm
            program(dve, Stages)

        @block.gpsimd
        def _(pool):
            G = nc.gpsimd

            class Stages:
                def split_windows():
                    pass

                def qk(b):
                    pass

                def stats(b):
                    pool.wait_ge(s["consts_set"], 1)
                    pool.wait_ge(s["mv1_done"], b + 1)
                    G.tensor_tensor(ve1[:], mv1[:, :, 1], eps[:], ALU.add).then_inc(s["ve1_done"], 1)
                    pool.wait_ge(s["ve1_done"], b + 1)
                    G.tensor_tensor(rstd1[:], ve1[:], neghalf[:], ALU.pow).then_inc(s["rstd1_done"], 1)

                def energy(b, t):
                    pass

                def scale(b, t):
                    pass

                def residual(r):
                    pool.wait_ge(s["res_mul"], 2 * r + 2)
                    if r < 2 * CLS:
                        dst = gu_r[r // CLS][:, r % CLS]
                    else:
                        if r == 2 * CLS:
                            pool.wait_ge(s["du_done"], 1)
                        dst = d_r[:, r - 2 * CLS]
                    G.tensor_tensor(dst, prod2[:, r % 2, 0], prod2[:, r % 2, 1], ALU.add).then_inc(s["res_done"], 1)

                def prob_t(b, t):
                    pass

                def split_x(b):
                    pass

                def coefficients(n):
                    pass

                def jumps():
                    pass

                def xm(b, t):
                    pool.wait_ge(s["mv2_done"], NT * b + t + 1)
                    G.tensor_tensor(ve2[:, t:t + 1], mv2[:, t, 1:2], eps[:, t:t + 1], ALU.add).then_inc(s["ve2_done"], 1)
                    pool.wait_ge(s["ve2_done"], NT * b + t + 1)
                    G.tensor_tensor(rstd2[:, t:t + 1], ve2[:, t:t + 1], neghalf[:, t:t + 1], ALU.pow).then_inc(s["rstd2_done"], 1)

                def norm_t(b, t):
                    pass

                def project(b):
                    pool.wait_ge(s["res_done"], 2 * CLS + MT)
                    pool.wait_ge(s["x1_added"], NT * (b + 1))
                    pool.wait_ge(s["out_stored"], 16 * NT * b)
                    G.tensor_tensor(xres[:], x[:], ones[:].broadcast_to([P, NT, HID]), ALU.mult).then_inc(s["x1_kept"], 1)

                def gate_up(b, m):
                    pool.wait_ge(s["ih_done"], MT * b + m + 1)
                    if m >= 2:
                        pool.wait_ge(s["zd_mm"], MT * b + m - 1)
                    G.tensor_tensor(il[:, m % 2], inter[:, m % 2], ih[:, m].bitcast(f32), ALU.subtract).then_inc(s["il_done"], 1)

                def down_basis(b, m):
                    pass

                def down_split(b, w):
                    pass

                def down(b, t):
                    pass

            program(pool, Stages)

        @block.tensor
        def _(pe):
            mm = nc.tensor.matmul

            class Stages:
                def split_windows():
                    pe.wait_ge(s["w_in"], 8 * 16)

                def qk(b):
                    pe.wait_ge(s["ctx_in"], 16 * (b + 1))
                    pe.wait_ge(s["xn2t_copied"], NT * b)
                    for n in range(2):
                        for c in range(CTX // P):
                            last = mm(abank[n][:], wqk[:, n, c], ctxT[:, c], start=c == 0, stop=c == CTX // P - 1)
                        last.then_inc(s["qk_mm"], 1)

                def stats(b):
                    pass

                def energy(b, t):
                    if t == 0:
                        pe.wait_ge(s["qk_done"], 2 * b + 2)
                    if t >= 2:
                        pe.wait_ge(s["exp_done"], NT * b + t - 1)
                    mm(abank[t % 2][:], qk_[:, 0, t * P:(t + 1) * P], qk_[:, 1], start=True, stop=True).then_inc(s["energy_mm"], 1)

                def scale(b, t):
                    pass

                def residual(r):
                    if r >= 2:
                        pe.wait_ge(s["res_mul"], 2 * (r - 1))
                    if r == 0:
                        pe.wait_ge(s["win_split"], 2)
                    if r == 2 * CLS:
                        pe.wait_ge(s["jump_split"], 2)
                    for k in range(2):
                        dst = bank[2 * (r % 2) + k][:]
                        if r < 2 * CLS:
                            p, c = 32 * (r // CLS), slice(r % CLS * HID, (r % CLS + 1) * HID)
                            pk = pick[p:p + 8, r % CLS, k]
                            mm(dst, pk, win_h[p:p + 8, c], start=True, stop=False)
                            last = mm(dst, pk, win_l[p:p + 8, c], start=False, stop=True)
                        else:
                            sp_ = spread[:, r - 2 * CLS]
                            mm(dst, sp_, jump[k][0], start=True, stop=False)
                            last = mm(dst, sp_, jump[k][1], start=False, stop=True)
                    last.then_inc(s["res_mm"], 1)

                def prob_t(b, t):
                    if t == 0:
                        pe.wait_ge(s["prob_done"], NT * (b + 1))
                    if t >= 2:
                        pe.wait_ge(s["pl_done"], NT * b + t - 1)
                    for m in range(NT):
                        last = nc.tensor.transpose(abank[t % 2][:, m * P:(m + 1) * P], prob[:, m, t * P:(t + 1) * P], ident[:])
                    last.then_inc(s["pT_mm"], 1)

                def split_x(b):
                    pass

                def coefficients(n):
                    pe.wait_ge(s["stack_done"], n + 1)
                    for g in range(4):
                        if 4 * n + g >= 2:
                            pe.wait_ge(s["stack_out"], 4 * n + g - 1)
                        for k in range(4):
                            if n < 2:
                                src = stack[:, (4 * g + k) * G_K:(4 * g + k + 1) * G_K]
                            else:
                                src = stack[:, (WIN * k + g) * P:(WIN * k + g + 1) * P]
                            last = nc.tensor.transpose(bank[4 + g % 2][0:src.shape[1], k * P:(k + 1) * P], src, ident[:])
                        last.then_inc(s["stack_mm"], 1)

                def jumps():
                    pass

                def xm(b, t):
                    if t == 0:
                        pe.wait_ge(s["xsplit_done"], b + 1)
                        pe.wait_ge(s["pl_done"], NT * (b + 1))
                    if t >= 2:
                        pe.wait_ge(s["xm_scaled"], NT * b + t - 1)
                    c = slice(t * P, (t + 1) * P)
                    for n in range(NT):
                        mm(abank[t % 2][:], xh[:, n, c], ph[:, n], start=n == 0, stop=False)
                        mm(abank[t % 2][:], xh[:, n, c], pl[:, n], start=False, stop=False)
                        last = mm(abank[t % 2][:], xl[:, n, c], ph[:, n], start=False, stop=n == NT - 1)
                    last.then_inc(s["xm_mm"], 1)

                def norm_t(b, t):
                    if t == 0:
                        pe.wait_ge(s["xn2_done"], NT * (b + 1))
                        pe.wait_ge(s["xm_scaled"], NT * (b + 1))
                    if t >= 2:
                        pe.wait_ge(s["xn2t_copied"], NT * b + t - 1)
                    for l in range(NT):
                        last = nc.tensor.transpose(abank[t % 2][:, l * P:(l + 1) * P], xn2[:, l, t * P:(t + 1) * P], ident[:])
                    last.then_inc(s["xn2T_mm"], 1)

                def project(b):
                    pe.wait_ge(s["xn2t_copied"], NT * (b + 1))
                    pe.wait_ge(s["zd_done"], WIN * b)
                    pe.wait_ge(s["stack_out"], 12)
                    for a in range(CLS):
                        last = mm(zgbank[0:G_K, :], g_basis[:, a], xn2T[:, a], start=a == 0, stop=a == CLS - 1)
                    last.then_inc(s["zg_mm"], 1)

                def gate_up(b, m):
                    w, a = m // CLS, m % CLS
                    if m == 0:
                        pe.wait_ge(s["zg_done"], b + 1)
                        pe.wait_ge(s["xn2r_done"], NT * (b + 1))
                        pe.wait_ge(s["res_done"], 2 * CLS + MT)
                        pe.wait_ge(s["out_added"], NT * b)
                    if m >= 2:
                        pe.wait_ge(s["mult_done"], MT * b + m - 1)
                    for n, (dst, done) in enumerate(((gbank, "g_mm"), (ubank, "u_mm"))):
                        mm(dst[m % 2][:], gu_r[n][:, a, w * P:(w + 1) * P], xn2r[:, a], start=True, stop=False)
                        mm(dst[m % 2][:], gu_v[n][:, m], zg, start=False, stop=True).then_inc(s[done], 1)

                def down_basis(b, m):
                    w, a = m // CLS, m % CLS
                    if a == 0 and w >= 2:
                        pe.wait_ge(s["zd_done"], WIN * b + w - 1)
                    if m == 0:
                        pe.wait_ge(s["du_done"], 1)
                    pe.wait_ge(s["il_done"], MT * b + m + 1)
                    u = d_u[:, m].rearrange("p k f -> p (k f)")
                    mm(zdbank[w][:], u, ih[:, m], start=a == 0, stop=False)
                    mm(zdbank[w][:], u, il[:, m % 2], start=False, stop=a == CLS - 1).then_inc(s["zd_mm"], 1)

                def down_split(b, w):
                    pass

                def down(b, t):
                    c = slice(t * P, (t + 1) * P)
                    for m in range(MT):
                        mm(obank[t][:], ih[:, m, c], d_r[:, m], start=m == 0, stop=False)
                    if t == 0:
                        pe.wait_ge(s["mult_done"], MT * (b + 1))
                        pe.wait_ge(s["zd_done"], WIN * (b + 1))
                    for w in range(WIN):
                        last = mm(obank[t][:], zd[:, w, c], d_v[:, w], start=False, stop=w == WIN - 1)
                    last.then_inc(s["out_mm"], 1)

            qk_ = qk
            program(pe, Stages)


def kernel(x, ctx_1024, L0_xattn_Wq, L0_xattn_bq, L0_xattn_Wk, L0_xattn_bk, L0_ffn_gate_cp, L0_ffn_up_cp, L0_ffn_down_cp):
    import concourse.bacc as bacc
    from concourse.bass_utils import run_bass_kernel_spmd

    c, at, hidden, _ = constants()
    x, ctx_1024, wq, bq, wk, bk, gate, up, down = (np.asarray(a) for a in (
        x, ctx_1024, L0_xattn_Wq, L0_xattn_bq, L0_xattn_Wk, L0_xattn_bk, L0_ffn_gate_cp, L0_ffn_up_cp, L0_ffn_down_cp))
    x, context = x[:, :, hidden], ctx_1024[:, hidden]

    def tiled(a):
        return a.reshape(*a.shape[:-2], -1, P, a.shape[-1]).swapaxes(-3, -2)

    arrays = dict(
        c, x=tiled(x), xT=tiled(x.swapaxes(1, 2)), ctxT=tiled(context.swapaxes(1, 2)),
        wqT=tiled(wq.T), wkT=tiled(wk.T), bq=bq.reshape(DK, 1), bk=bk.reshape(DK, 1),
        g_node=gate[at["g_node"]].reshape(P, -1), u_node=up[at["g_node"]].reshape(P, -1),
        g_win=gate[at["g_win"]], u_win=up[at["g_win"]],
        d_node=down[at["d_node"]].reshape(P, -1), d_knot=down[at["d_knot"]].reshape(D_CELLS, -1))
    arrays = {f"in_{k}": np.ascontiguousarray(v) for k, v in arrays.items()}
    nc = bacc.Bacc("TRN2", target_bir_lowering=False, num_devices=1)
    d = {k[3:]: nc.dram_tensor(k, v.shape, mybir.dt.from_np(v.dtype), kind="ExternalInput").ap() for k, v in arrays.items()}
    out = nc.dram_tensor("out", (B, NT, P, HID), mybir.dt.float32, kind="ExternalOutput").ap()
    xattn_spline_ffn_kernel(nc, d, out)
    got = run_bass_kernel_spmd(nc, [arrays], core_ids=[0]).results[0]["out"]
    back = np.argsort(hidden)
    return np.ascontiguousarray(got.reshape(B, TOK, HID)[:, :, back])
```

```python
import numpy as np
import concourse.bass as bass
from concourse import mybir
from contextlib import ExitStack

BF16 = mybir.dt.np(mybir.dt.bfloat16)
B, TOK, HID, CTX, DK, INTER = 4, 512, 512, 256, 128, 2048
NCTRL = int(INTER * HID / 128.9)
STEP = (NCTRL - 1) / (INTER * HID - 1)
PERIOD = 1 / STEP
P = 128
NT = HID // P
CLS = 4
MT = INTER // P
G_NODES = 4 * CLS + 1
G_FN = 2 * G_NODES
G_K = 3 * G_FN
WIN = 4
D_NODES = 16
D_FN = 2 * D_NODES
D_CELLS = WIN * (D_NODES - 1)
LAG = 3
HALF = 64
WIDTH = PERIOD / 4
S2, S3 = 256.0, 2048.0
EPS = 1e-5


def hermite(u):
    return 2 * u**3 - 3 * u**2 + 1, u**3 - 2 * u**2 + u, 3 * u**2 - 2 * u**3, u**3 - u**2


def basis_at(pos, nodes):
    c = np.clip(np.searchsorted(nodes, pos, side="right") - 1, 0, len(nodes) - 2)
    width = nodes[c + 1] - nodes[c]
    out = np.zeros((len(pos), 2 * len(nodes)))
    for k, h in enumerate(hermite((pos - nodes[c]) / width)):
        out[np.arange(len(pos)), 2 * c + k] = h * (width / WIDTH if k % 2 else 1)
    return out, c


def node_taps(t):
    k = np.floor(t).astype(np.int64)
    f = t - k
    value = 0.5 * np.stack([-f + 2 * f**2 - f**3, 2 - 5 * f**2 + 3 * f**3, f + 4 * f**2 - 3 * f**3, f**3 - f**2], -1)
    slope = 0.5 * np.stack([4 * f - 1 - 3 * f**2, 9 * f**2 - 10 * f, 1 + 8 * f - 9 * f**2, 3 * f**2 - 2 * f], -1)
    return control(k[..., None] + np.arange(-1, 3)), np.stack([value, slope * (WIDTH * STEP)], -2)


def control(k):
    return np.clip(k, 0, NCTRL - 1)


def cell_residual(pos, left, right, knot):
    inside = (knot > left) & (knot < right)
    knot = np.where(inside, knot, right)
    width = right - left
    _, _, value, slope = hermite((pos - left) / width)
    x, e = np.maximum(pos - knot, 0) * STEP, (right - knot) * STEP
    r2 = x**2 - (value * e**2 + slope * 2 * e * width * STEP)
    r3 = x**3 - (value * e**3 + slope * 3 * e**2 * width * STEP)
    return np.where(inside, r2, 0) * S2, np.where(inside, r3, 0) * S3


def gate_layout():
    start = np.arange(INTER) * HID * STEP
    first = PERIOD * (1 - (start - np.floor(start)))
    for offset in np.arange(-4.7, 0, 0.1):
        turn = (first - offset) % PERIOD
        order = np.sort(turn)
        edge = np.array([0] + [order[a * HID - 1:a * HID + 1].mean() for a in range(1, CLS)])
        nodes = np.append((offset + np.arange(4)[:, None] * PERIOD + edge).ravel(), offset + 4 * PERIOD)
        cell = np.searchsorted(nodes, np.arange(HID), side="right") - 1
        if nodes[-1] >= HID - 1 and (np.bincount(cell % CLS) == P).all():
            break
    else:
        raise ValueError("no layout with equal classes")
    cls = np.searchsorted(edge, turn, side="right") - 1
    hidden = np.argsort(cell % CLS, kind="stable")
    rows = np.stack([np.flatnonzero(cls == a) for a in range(CLS)]).reshape(CLS, WIN, P)
    knot = np.rint(start + (offset + turn) * STEP).astype(np.int64)
    return nodes, cell, hidden, rows, knot, start


def constants():
    nodes, cell, hidden, rows, knot, start = gate_layout()
    c, at = {}, {}
    tiles = rows.transpose(1, 0, 2).reshape(MT, P)
    idx, coef = node_taps(start[tiles.T][:, :, None] + nodes * STEP)
    at["g_node"] = idx.reshape(P, MT * G_NODES, 4)
    c["g_coef"] = coef.reshape(P, MT * G_NODES * 8).astype(np.float32)
    u = basis_at(hidden.astype(float), nodes)[0].reshape(CLS, P, G_FN)
    c["g_basis"] = np.tile(u.transpose(1, 0, 2)[:, :, None], (1, 1, 3, 1)).reshape(P, CLS * G_K).astype(np.float32)
    lo = (np.arange(G_K) // G_FN) == 1
    c["g_low"] = np.where(lo, -1.0, 0.0).reshape(G_K, 1).astype(np.float32)
    byclass = rows.reshape(INTER)
    win = np.zeros((32, INTER), np.int64)
    win[:8] = control(knot[byclass] + np.arange(-2, 6)[:, None])
    at["g_win"] = win
    jump = {2: np.array([0.5, -1, 0, 1, -0.5]), 3: np.array([0.5, -2, 3, -2, 0.5])}
    pick = np.zeros((32, CLS, 2, P))
    r2, r3 = np.zeros((P, INTER)), np.zeros((P, INTER))
    for a in range(CLS):
        h = hidden[a * P:(a + 1) * P]
        for n in range(4):
            pick[n:n + 5, a, 0, cell[h] // CLS == n] = jump[2][:, None] / S2
            pick[n:n + 5, a, 1, cell[h] // CLS == n] = jump[3][:, None] / S3
        i = rows[a].ravel()
        place = ((knot[i] + (cell[h] // CLS)[:, None]) - start[i]) * PERIOD
        left, right = nodes[cell[h]][:, None], nodes[cell[h] + 1][:, None]
        r2[:, a * HID:(a + 1) * HID], r3[:, a * HID:(a + 1) * HID] = cell_residual(h[:, None], left, right, place)
    c["g_pick"] = np.tile(pick.reshape(32, CLS * 2 * P), (4, 1)).astype(BF16)
    c["g_winlow"] = np.where(np.arange(P) // 32 % 2 == 1, -1.0, 0.0).reshape(P, 1).astype(np.float32)
    c["g_r2"], c["g_r3"] = r2.astype(np.float16), r3.astype(np.float16)
    window = tiles.reshape(WIN, CLS * P)
    dn = np.stack([np.linspace(w.min(), w.max(), D_NODES) for w in window])
    t = hidden.reshape(NT, P).T[:, :, None] * (INTER * STEP) + dn.ravel() * STEP
    idx, coef = node_taps(t)
    at["d_node"] = idx.reshape(P, NT * WIN * D_NODES, 4)
    c["d_coef"] = coef.reshape(P, NT * WIN * D_NODES * 8).astype(np.float32)
    basis, spread = np.zeros((P, MT, D_FN)), np.zeros((HALF, MT, P))
    left, right = dn[:, :-1].ravel(), dn[:, 1:].ravel()
    row0 = hidden * (INTER * STEP)
    kd = np.floor(row0 + right[:, None] * STEP).astype(np.int64)
    at["d_knot"] = np.zeros((2, HALF, 5, HID), np.int64)
    at["d_knot"][:, :D_CELLS] = control(kd[:, None] + np.arange(-2, 3)[:, None])
    place = (kd - row0) * PERIOD
    r2, r3 = np.zeros((P, MT, HID)), np.zeros((P, MT, HID))
    for m in range(MT):
        basis[:, m], k = basis_at(tiles[m].astype(float), dn[m // CLS])
        k = k + (m // CLS) * (D_NODES - 1)
        spread[k, m, np.arange(P)] = 1
        r2[:, m], r3[:, m] = cell_residual(tiles[m][:, None], left[k][:, None], right[k][:, None], place[k])
    c["d_basis"] = basis.reshape(P, MT * D_FN).astype(np.float32)
    c["d_spread"] = np.tile(spread.reshape(HALF, INTER), (2, 1)).astype(BF16)
    c["d_r2"], c["d_r3"] = (r.reshape(P, 4, 4 * HID).transpose(1, 0, 2).astype(np.float16) for r in (r2, r3))
    c["d_low"] = np.where(np.arange(P) // D_FN == 1, -1.0, 0.0).reshape(P, 1).astype(np.float32)
    c["ident"] = np.eye(P, dtype=np.float32)
    return c, at, hidden, tiles


def xattn_spline_ffn_kernel(nc: bass.Bass, d, out: bass.AP):
    f32, f32r, bf16, fp16 = mybir.dt.float32, mybir.dt.float32r, mybir.dt.bfloat16, mybir.dt.float16
    ALU, ACT, AX = mybir.AluOpType, mybir.ActivationFunctionType, mybir.AxisListType

    ctx = ExitStack()
    with ctx:
        def sb(name, shape, dt, stack=ctx):
            return stack.enter_context(nc.sbuf_tensor(name, shape, dt))

        def sem(name):
            return ctx.enter_context(nc.semaphore(name))

        wqk = sb("wqk", [P, 2, CTX // P, DK], f32)
        bqk = sb("bqk", [DK, 2], f32)
        ident = sb("ident", [P, P], f32)
        g_basis = sb("g_basis", [P, CLS, G_K], f32)
        g_low = sb("g_low", [G_K, 1], f32)
        d_low = sb("d_low", [P, 1], f32)
        g_winlow = sb("g_winlow", [P, 1], f32)
        neghalf = sb("neghalf", [P, NT], f32)
        eps = sb("eps", [P, NT], f32)
        ones = sb("ones", [P, 1, 1], f32)
        gu_r = [sb(f"{n}_r", [P, CLS, WIN * P], f32r) for n in ("gate", "up")]
        gu_v = [sb(f"{n}_v", [G_K, MT, P], f32r) for n in ("gate", "up")]
        d_v = sb("d_v", [P, WIN, HID], f32r)
        d_u = sb("d_u", [P, MT, 4, D_FN], f32r)
        ctxT = sb("ctxT", [P, CTX // P, TOK], f32)
        qk = sb("qk", [P, 2, TOK], f32)
        x = sb("x", [P, NT, HID], f32)
        xT = sb("xT", [P, NT, TOK], f32)
        xh = sb("xh", [P, NT, TOK], f32r)
        xl = sb("xl", [P, NT, TOK], f32r)
        prob = sb("prob", [P, NT, TOK], f32)
        ph = sb("ph", [P, NT, TOK], f32r)
        pl = sb("pl", [P, NT, TOK], f32r)
        nmax = sb("nmax", [P, NT], f32)
        rsum = sb("rsum", [P, NT], f32)
        rinv = sb("rinv", [P, NT], f32)
        bst1, bst2 = sb("bst1", [P, NT, 6], f32), sb("bst2", [P, NT, 6], f32)
        mv1, mv2 = sb("mv1", [P, NT, 2], f32), sb("mv2", [P, NT, 2], f32)
        ve1, ve2 = sb("ve1", [P, NT], f32), sb("ve2", [P, NT], f32)
        rstd1, rstd2 = sb("rstd1", [P, NT], f32), sb("rstd2", [P, NT], f32)
        nmr1 = sb("nmr1", [P, NT], f32)
        xn2, xn2T, xn2r, xm = xT, prob, xh, qk

        prep = ExitStack()
        coef = sb("coef", [P, MT * G_NODES * 8], f32, prep)
        taps = [sb(f"taps{n}", [P, MT * G_NODES * 4], f32, prep) for n in range(2)]
        prod = sb("prod", [P, MT * G_NODES * 8], f32, prep)
        fval = sb("fval", [P, MT * G_FN], f32, prep)
        sb("pad", [P, (32768 - 4 * (MT * G_NODES * (8 + 4 + 4 + 8) + MT * G_FN)) // 4], f32, prep)
        stack = sb("stack", [P, 2048], f32, prep)
        prod2 = sb("prod2", [P, 2, 2, HID], f32, prep)
        work = sb("work", [P, 6144], f32, prep)
        pick = sb("pick", [P, CLS, 2, P], bf16, prep)
        knots = sb("knots", [P, 5, HID], f32, prep)
        spread = sb("spread", [P, MT, P], bf16, prep)
        prep.close()
        d_r = sb("d_r", [P, MT, HID], f32r)
        ih = sb("ih", [P, MT, TOK], f32r)
        xres = sb("xres", [P, NT, HID], f32)
        inter = sb("inter", [P, 3, TOK], f32)
        il = sb("il", [P, 2, TOK], f32r)
        zd = sb("zd", [P, WIN, TOK], f32r)
        zg = zd[0:G_K, WIN - 1, :]

        r2g, r3g = (work[:, n * 1024:(n + 1) * 1024].bitcast(fp16) for n in range(2))
        win = work[:, 2048:4096]
        win_h, win_hl = (work[:, 4096 + n * 1024:5120 + n * 1024].bitcast(bf16) for n in range(2))
        rd = [[work[:, s * 2048 + n * 1024:s * 2048 + (n + 1) * 1024].bitcast(fp16) for n in range(2)] for s in range(3)]
        ja, jb = (stack[:, n * 512:(n + 1) * 512] for n in range(2))
        jump = [stack[:, 1024 + n * 256:1280 + n * 256].bitcast(bf16) for n in range(2)]

        bank = [ctx.enter_context(nc.psum_tensor(f"bank{n}", [P, 512], f32)) for n in range(8)]
        gbank, ubank, obank = bank[0:2], bank[2:4], bank[0:4]
        zgbank, zdbank = bank[4], [bank[5], bank[4], bank[5], bank[4]]
        abank = bank[6:8]

        names = """w_in ctx_in x_in xt_in win_in r_in node_in coefg_in upnode_in coefd_in dnode_in dbasis_in knot_in
            rd0_in rd1_in rd2_in out_stored
            consts_set win_hi win_split jump_a jump_b jump_d jump_hi jump_split res_mm res_mul res_done
            tap_mul tap_sum stack_hi stack_done stack_mm stack_out du_hi du_done
            qk_mm qk_done energy_mm max_done exp_done rinv_done prob_done pT_mm ph_done pl_done
            stats1 mv1_done ve1_done rstd1_done nmr_done xh_done xsplit_done xm_mm xm_scaled x1_added
            stats2 mv2_done ve2_done rstd2_done xn2_done xn2T_mm xn2t_copied xn2r_done
            x1_kept zg_mm zg_hi zg_done g_mm u_mm silu_done mult_done ih_done il_done zd_mm zd_hi zd_done
            out_mm out_added"""
        s = {n: sem(n) for n in names.split()}

        def attention_only(st):
            st.split_windows()
            st.qk(0)
            st.stats(0)
            for t in range(NT):
                st.energy(0, t)
            st.softmax(0)
            st.mean_shift(0)
            st.scale(0)
            for r in range(2 * CLS):
                st.residual(r)
            for t in range(NT):
                st.prob_t(0, t)
            st.split_x(0)
            for n in range(2):
                st.coefficients(n)
            for t in range(NT):
                st.xm(0, t)
            st.coefficients(2)
            st.jumps()
            for r in range(2 * CLS, 2 * CLS + MT):
                st.residual(r)
            for t in range(NT):
                st.norm_t(0, t)

        def ffn(st, b, a=None):
            st.project(b)
            if a is not None:
                st.qk(a)
            for m in range(MT):
                st.gate_up(b, m)
                if m >= LAG:
                    st.down_basis(b, m - LAG)
                    if (m - LAG) % CLS == CLS - 1:
                        st.down_split(b, (m - LAG) // CLS)
                if a is not None:
                    if m == 1:
                        st.energy(a, 0)
                        st.energy(a, 1)
                        st.softmax(a)
                    if m == 2:
                        st.energy(a, 2)
                        st.energy(a, 3)
                    if m == 5:
                        st.scale(a)
                    if 8 <= m < 8 + NT:
                        st.prob_t(a, m - 8)
            if a is not None:
                st.split_x(a)
            st.down(b, 0, range(MT - LAG))
            for m in range(MT - LAG, MT):
                st.down_basis(b, m)
            st.down_split(b, WIN - 1)
            st.down(b, 0, range(MT - LAG, MT))
            st.down(b, 1, range(MT))
            if a is not None:
                st.stats(a)
            st.down_tail(b, 0)
            if a is not None:
                st.mean_shift(a)
                for t in range(NT):
                    st.xm(a, t)
            st.down_tail(b, 1)
            st.down(b, 2, range(MT))
            st.down_tail(b, 2)
            if a is not None:
                for t in range(NT):
                    st.norm_t(a, t)
            st.down(b, 3, range(MT))
            st.down_tail(b, 3)

        def program(eng, st):
            attention_only(st)
            with eng.Fori(0, B - 1) as b:
                ffn(st, b, b + 1)
            ffn(st, B - 1)

        block = ctx.enter_context(nc.Block())

        @block.sync
        def _(sp):
            def load(dst, name, signal):
                sp.dma_start(dst, d[name]).then_inc(s[signal], 16)

            load(wqk[:, 0], "wqT", "w_in")
            load(wqk[:, 1], "wkT", "w_in")
            load(bqk[:, 0:1], "bq", "w_in")
            load(bqk[:, 1:2], "bk", "w_in")
            load(ident[:], "ident", "w_in")
            sp.dma_start(ctxT[:], d["ctxT"][0]).then_inc(s["ctx_in"], 16)
            for n, name in enumerate(("g_win", "g_win", "u_win", "u_win")):
                load(win[32 * n:32 * n + 32, :], name, "win_in")
            load(pick[:].rearrange("p a k n -> p (a k n)"), "g_pick", "win_in")
            load(g_winlow[:], "g_winlow", "win_in")
            load(r2g, "g_r2", "r_in")
            load(r3g, "g_r3", "r_in")
            sp.dma_start(x[:], d["x"][0]).then_inc(s["x_in"], 16)
            sp.dma_start(xT[:], d["xT"][0]).then_inc(s["xt_in"], 16)
            load(coef[:], "g_coef", "coefg_in")
            load(taps[0][:], "g_node", "node_in")
            load(taps[1][:], "u_node", "upnode_in")
            load(g_basis[:].rearrange("p a n -> p (a n)"), "g_basis", "w_in")
            load(g_low[:], "g_low", "w_in")
            load(d_low[:], "d_low", "w_in")
            load(knots[:].rearrange("p w n -> p (w n)"), "d_knot", "knot_in")
            load(spread[:].rearrange("p m n -> p (m n)"), "d_spread", "knot_in")
            sp.wait_ge(s["res_mul"], 16)
            for n in range(2):
                sp.dma_start(rd[0][n], d[f"d_r{n + 2}"][0]).then_inc(s["rd0_in"], 16)
                sp.dma_start(rd[1][n], d[f"d_r{n + 2}"][1]).then_inc(s["rd1_in"], 16)
                sp.dma_start(rd[2][n], d[f"d_r{n + 2}"][2]).then_inc(s["rd2_in"], 16)
            sp.wait_ge(s["tap_mul"], 2)
            load(coef[:, 0:NT * WIN * D_NODES * 8], "d_coef", "coefd_in")
            load(taps[0][:, 0:NT * WIN * D_NODES * 4], "d_node", "dnode_in")
            load(taps[1][:, 0:MT * D_FN], "d_basis", "dbasis_in")
            sp.wait_ge(s["res_mul"], 2 * (2 * CLS + 4))
            for n in range(2):
                sp.dma_start(rd[0][n], d[f"d_r{n + 2}"][3]).then_inc(s["rd0_in"], 16)

            def store(b, t):
                sp.wait_ge(s["out_added"], NT * b + t + 1)
                sp.dma_start(out[bass.ds(b, 1), t].rearrange("a p n -> (a p) n"), xres[:, t]).then_inc(s["out_stored"], 16)

            def fetch(src, b):
                return d[src][bass.ds(b, 1)].rearrange("a p t n -> (a p) t n")

            with sp.Fori(0, B - 1) as b:
                if True:
                    sp.wait_ge(s["qk_mm"], 2 * b + 2)
                    sp.dma_start(ctxT[:], fetch("ctxT", b + 1)).then_inc(s["ctx_in"], 16)
                    sp.wait_ge(s["xn2_done"], NT * (b + 1))
                    sp.wait_ge(s["x1_kept"], b + 1)
                    sp.dma_start(x[:], fetch("x", b + 1)).then_inc(s["x_in"], 16)
                    sp.wait_ge(s["xn2T_mm"], NT * (b + 1))
                    sp.dma_start(xT[:], fetch("xT", b + 1)).then_inc(s["xt_in"], 16)
                for t in range(NT):
                    store(b, t)
            for t in range(NT):
                store(B - 1, t)
            sp.wait_ge(s["out_stored"], 16 * NT * B + 1)

        @block.scalar
        def _(act):
            class Stages:
                def split_windows():
                    act.wait_ge(s["win_in"], 6 * 16)
                    nc.scalar.activation(win_h, win, ACT.Copy).then_inc(s["win_hi"], 1)

                def qk(b):
                    for n in range(2):
                        act.wait_ge(s["qk_mm"], 2 * b + n + 1)
                        if n == 0:
                            act.wait_ge(s["w_in"], 8 * 16)
                            if not (isinstance(b, int) and b == 0):
                                act.wait_ge(s["x1_added"], NT * b)
                        nc.scalar.activation(qk_[:, n], abank[n][:], ACT.Identity, bias=bqk[:, n:n + 1]).then_inc(s["qk_done"], 1)

                def stats(b):
                    pass

                def energy(b, t):
                    pass

                def softmax(b):
                    for t in range(NT):
                        act.wait_ge(s["max_done"], NT * b + t + 1)
                        if t == 0 and not (isinstance(b, int) and b == 0):
                            act.wait_ge(s["zg_mm"], b)
                        nc.scalar.activation(prob[:, t], abank[t % 2][:], ACT.Exp, bias=nmax[:, t:t + 1],
                                             accum_out=rsum[:, t:t + 1]).then_inc(s["exp_done"], 1)

                def mean_shift(b):
                    pass

                def scale(b):
                    pass

                def residual(r):
                    pass

                def prob_t(b, t):
                    act.wait_ge(s["pT_mm"], NT * b + t + 1)
                    nc.scalar.activation(ph[:, t], abank[t % 2][:], ACT.Copy).then_inc(s["ph_done"], 1)

                def split_x(b):
                    pass

                def coefficients(n):
                    act.wait_ge(s["tap_sum"], n + 1)
                    if n:
                        act.wait_ge(s["stack_mm"], 4 * n)
                    if n < 2:
                        st3 = stack[:, 0:MT * G_K].bitcast(f32r).rearrange("p (m k f) -> p m k f", m=MT, k=3)
                        v = fval[:].rearrange("p (m f) -> p m f", m=MT)
                        slots = (0, 1)
                    else:
                        st3 = stack[:].bitcast(f32r).rearrange("p (m k f) -> p m k f", m=NT * WIN, k=4)
                        v = fval[:, 0:NT * WIN * D_FN].rearrange("p (m f) -> p m f", f=D_FN)
                        slots = (0, 1, 2)
                    for k in slots:
                        last = nc.scalar.activation(st3[:, :, k], v, ACT.Copy)
                    last.then_inc(s["stack_hi"], 1)
                    for g in range(4):
                        act.wait_ge(s["stack_mm"], 4 * n + g + 1)
                        if n < 2:
                            dst = gu_v[n][:, 4 * g:4 * g + 4].rearrange("p m i -> p (m i)")
                        else:
                            dst = d_v[:, g]
                        nc.scalar.activation(dst, bank[4 + g % 2][0:dst.shape[0], :], ACT.Copy).then_inc(s["stack_out"], 1)
                    if n == 2:
                        act.wait_ge(s["dbasis_in"], 16)
                        u = taps[1][:, 0:MT * D_FN].rearrange("p (m f) -> p m f", m=MT)
                        for k in (0, 1, 3):
                            last = nc.scalar.activation(d_u[:, :, k], u, ACT.Copy)
                        last.then_inc(s["du_hi"], 1)

                def jumps():
                    for k in range(2):
                        act.wait_ge(s["jump_d"], k + 1)
                        nc.scalar.activation(jump[k], ja, ACT.Copy).then_inc(s["jump_hi"], 1)

                def xm(b, t):
                    act.wait_ge(s["xm_mm"], NT * b + t + 1)
                    if t == 0:
                        act.wait_ge(s["nmr_done"], b + 1)
                    if t >= 2:
                        act.wait_ge(s["x1_added"], NT * b + t - 1)
                    nc.scalar.activation(xm_[:, t % 2], abank[t % 2][:], ACT.Identity, bias=nmr1[:, t:t + 1],
                                         scale=rstd1[:, t:t + 1]).then_inc(s["xm_scaled"], 1)

                def norm_t(b, t):
                    act.wait_ge(s["xn2T_mm"], NT * b + t + 1)
                    nc.scalar.activation(xn2T[:, t], abank[t % 2][:], ACT.Copy).then_inc(s["xn2t_copied"], 1)

                def project(b):
                    act.wait_ge(s["zg_mm"], b + 1)
                    if isinstance(b, int) and b == 0 or not isinstance(b, int):
                        act.wait_ge(s["res_done"], 2 * CLS + MT)
                    nc.scalar.activation(zg, zgbank[0:G_K, :], ACT.Copy).then_inc(s["zg_hi"], 1)

                def gate_up(b, m):
                    act.wait_ge(s["g_mm"], MT * b + m + 1)
                    if m >= 3:
                        act.wait_ge(s["il_done"], MT * b + m - 2)
                    nc.scalar.activation(inter[:, m % 3], gbank[m % 2][:], ACT.Silu).then_inc(s["silu_done"], 1)

                def down_basis(b, m):
                    pass

                def down_split(b, w):
                    act.wait_ge(s["zd_mm"], MT * b + CLS * (w + 1))
                    nc.scalar.activation(zd[:, w], zdbank[w][:], ACT.Copy).then_inc(s["zd_hi"], 1)

                def down(b, t, tiles):
                    pass

                def down_tail(b, t):
                    pass

            qk_, xm_ = qk, xm
            program(act, Stages)

        @block.vector
        def _(dve):
            V = nc.vector

            class Stages:
                def split_windows():
                    V.memset(eps[:], EPS)
                    V.memset(ones[:], 1.0).then_inc(s["out_stored"], 1)
                    V.memset(neghalf[:], -0.5).then_inc(s["consts_set"], 1)
                    dve.wait_ge(s["win_hi"], 1)
                    V.scalar_tensor_tensor(win_hl, win_h, g_winlow[:], win, ALU.mult, ALU.add).then_inc(s["win_split"], 1)

                def qk(b):
                    pass

                def stats(b):
                    dve.wait_ge(s["x_in"], 16 * (b + 1))
                    for t in range(NT):
                        last = V.bn_stats(bst1[:, t], x[:, t])
                    last.then_inc(s["stats1"], 1)
                    dve.wait_ge(s["consts_set"], 1)
                    dve.wait_ge(s["stats1"], b + 1)
                    for t in range(NT):
                        last = V.bn_aggr(mv1[:, t], bst1[:, t])
                    last.then_inc(s["mv1_done"], 1)

                def mean_shift(b):
                    dve.wait_ge(s["rstd1_done"], b + 1)
                    V.scalar_tensor_tensor(nmr1[:], mv1[:, :, 0], -1.0, rstd1[:], ALU.mult, ALU.mult).then_inc(s["nmr_done"], 1)

                def energy(b, t):
                    pass

                def softmax(b):
                    for t in range(NT):
                        dve.wait_ge(s["energy_mm"], NT * b + t + 1)
                        V.tensor_reduce(nmax[:, t:t + 1], abank[t % 2][:], AX.X, ALU.max, negate=True).then_inc(s["max_done"], 1)

                def scale(b):
                    dve.wait_ge(s["exp_done"], NT * (b + 1))
                    V.reciprocal(rinv[:], rsum[:]).then_inc(s["rinv_done"], 1)
                    dve.wait_ge(s["rinv_done"], b + 1)
                    for t in range(NT):
                        V.tensor_scalar(prob[:, t], prob[:, t], rinv[:, t:t + 1], None, ALU.mult).then_inc(s["prob_done"], 1)

                def residual(r):
                    dve.wait_ge(s["res_mm"], r + 1)
                    if r == 0:
                        dve.wait_ge(s["r_in"], 32)
                    if r >= 2:
                        dve.wait_ge(s["res_done"], r - 1)
                    if r < 2 * CLS:
                        c = slice(r % CLS * HID, (r % CLS + 1) * HID)
                        parts = r2g[:, c], r3g[:, c]
                    else:
                        m = r - 2 * CLS
                        if m % 4 == 0:
                            dve.wait_ge(s[f"rd{m // 4 % 3}_in"], 32 * (m // 12 + 1))
                        parts = (rd[m // 4 % 3][n][:, m % 4 * HID:(m % 4 + 1) * HID] for n in range(2))
                    for k, part in enumerate(parts):
                        V.tensor_tensor(prod2[:, r % 2, k], bank[2 * (r % 2) + k][:], part, ALU.mult).then_inc(s["res_mul"], 1)

                def prob_t(b, t):
                    dve.wait_ge(s["ph_done"], NT * b + t + 1)
                    V.tensor_tensor(pl[:, t], abank[t % 2][:], ph[:, t].bitcast(f32), ALU.subtract).then_inc(s["pl_done"], 1)

                def split_x(b):
                    dve.wait_ge(s["xt_in"], 16 * (b + 1))
                    dve.wait_ge(s["u_mm"], MT * b)
                    V.tensor_copy(xh[:], xT[:]).then_inc(s["xh_done"], 1)
                    dve.wait_ge(s["xh_done"], b + 1)
                    V.tensor_tensor(xl[:], xT[:], xh[:].bitcast(f32), ALU.subtract).then_inc(s["xsplit_done"], 1)

                def coefficients(n):
                    for need, count in ((("coefg_in", 16), ("node_in", 16)), (("upnode_in", 16),),
                                        (("coefd_in", 16), ("dnode_in", 16)))[n]:
                        dve.wait_ge(s[need], count)
                    nodes = MT * G_NODES if n < 2 else NT * WIN * D_NODES
                    if n:
                        dve.wait_ge(s["stack_hi"], n)
                    c = coef[:, 0:nodes * 8].rearrange("p (n v t) -> p n v t", v=2, t=4)
                    tp = taps[n % 2][:, 0:nodes * 4].rearrange("p (n a t) -> p n a t", a=1, t=4).broadcast_to([P, nodes, 2, 4])
                    pr = prod[:, 0:nodes * 8]
                    V.tensor_tensor(pr.rearrange("p (n v t) -> p n v t", v=2, t=4), c, tp, ALU.mult).then_inc(s["tap_mul"], 1)
                    dve.wait_ge(s["tap_mul"], n + 1)
                    V.tensor_reduce(fval[:, 0:nodes * 2], pr.rearrange("p (n t) -> p n t", t=4), AX.X, ALU.add).then_inc(s["tap_sum"], 1)
                    dve.wait_ge(s["stack_hi"], n + 1)
                    if n < 2:
                        st3 = stack[:, 0:MT * G_K].rearrange("p (m k f) -> p m k f", m=MT, k=3)
                        v, lo = fval[:].rearrange("p (m f) -> p m f", m=MT), 2
                    else:
                        st3 = stack[:].rearrange("p (m k f) -> p m k f", m=NT * WIN, k=4)
                        v, lo = fval[:, 0:NT * WIN * D_FN].rearrange("p (m f) -> p m f", f=D_FN), 3
                    V.tensor_tensor(st3[:, :, lo].bitcast(f32r), v, st3[:, :, 0], ALU.subtract).then_inc(s["stack_done"], 1)
                    if n == 2:
                        dve.wait_ge(s["du_hi"], 1)
                        u = taps[1][:, 0:MT * D_FN].rearrange("p (m f) -> p m f", m=MT)
                        V.tensor_tensor(d_u[:, :, 2], u, d_u[:, :, 0].bitcast(f32), ALU.subtract).then_inc(s["du_done"], 1)

                def jumps():
                    dve.wait_ge(s["knot_in"], 32)
                    dve.wait_ge(s["stack_mm"], 12)
                    k0, k1, k2, k3, k4 = (knots[:, w] for w in range(5))
                    V.tensor_tensor(ja, k0, k4, ALU.subtract)
                    V.tensor_tensor(jb, k1, k3, ALU.subtract).then_inc(s["jump_a"], 1)
                    dve.wait_ge(s["jump_a"], 1)
                    V.tensor_scalar(ja, ja, 0.5 / S2, None, ALU.mult).then_inc(s["jump_b"], 1)
                    dve.wait_ge(s["jump_b"], 1)
                    V.scalar_tensor_tensor(ja, jb, -1 / S2, ja, ALU.mult, ALU.add).then_inc(s["jump_d"], 1)
                    dve.wait_ge(s["jump_hi"], 1)
                    V.tensor_tensor(jump[0][HALF:P], ja[HALF:P], jump[0][HALF:P], ALU.subtract).then_inc(s["jump_split"], 1)
                    dve.wait_ge(s["jump_split"], 1)
                    V.tensor_tensor(ja, k0, k4, ALU.add)
                    V.tensor_tensor(jb, k1, k3, ALU.add).then_inc(s["jump_a"], 1)
                    dve.wait_ge(s["jump_a"], 2)
                    V.tensor_scalar(ja, ja, 0.5 / S3, None, ALU.mult).then_inc(s["jump_b"], 1)
                    dve.wait_ge(s["jump_b"], 2)
                    V.scalar_tensor_tensor(ja, jb, -2 / S3, ja, ALU.mult, ALU.add).then_inc(s["jump_b"], 1)
                    dve.wait_ge(s["jump_b"], 3)
                    V.scalar_tensor_tensor(ja, k2, 3 / S3, ja, ALU.mult, ALU.add).then_inc(s["jump_d"], 1)
                    dve.wait_ge(s["jump_hi"], 2)
                    V.tensor_tensor(jump[1][HALF:P], ja[HALF:P], jump[1][HALF:P], ALU.subtract).then_inc(s["jump_split"], 1)

                def xm(b, t):
                    dve.wait_ge(s["xm_scaled"], NT * b + t + 1)
                    V.tensor_tensor(x[:, t], x[:, t], xm_[:, t % 2], ALU.add).then_inc(s["x1_added"], 1)
                    dve.wait_ge(s["x1_added"], NT * b + t + 1)
                    V.bn_stats(bst2[:, t], x[:, t]).then_inc(s["stats2"], 1)
                    dve.wait_ge(s["consts_set"], 1)
                    dve.wait_ge(s["stats2"], NT * b + t + 1)
                    V.bn_aggr(mv2[:, t], bst2[:, t]).then_inc(s["mv2_done"], 1)
                    if t:
                        normalise(b, t - 1)
                    if t == NT - 1:
                        normalise(b, t)

                def norm_t(b, t):
                    dve.wait_ge(s["xn2t_copied"], NT * b + t + 1)
                    V.tensor_copy(xn2r[:, t], xn2T[:, t]).then_inc(s["xn2r_done"], 1)

                def project(b):
                    dve.wait_ge(s["zg_hi"], b + 1)
                    dve.wait_ge(s["w_in"], 8 * 16)
                    V.scalar_tensor_tensor(zg, zg.bitcast(f32), g_low[:], zgbank[0:G_K, :], ALU.mult, ALU.add).then_inc(s["zg_done"], 1)

                def gate_up(b, m):
                    dve.wait_ge(s["silu_done"], MT * b + m + 1)
                    dve.wait_ge(s["u_mm"], MT * b + m + 1)
                    V.tensor_tensor(inter[:, m % 3], inter[:, m % 3], ubank[m % 2][:], ALU.mult).then_inc(s["mult_done"], 1)
                    dve.wait_ge(s["mult_done"], MT * b + m + 1)
                    V.tensor_copy(ih[:, m], inter[:, m % 3]).then_inc(s["ih_done"], 1)

                def down_basis(b, m):
                    pass

                def down_split(b, w):
                    dve.wait_ge(s["zd_hi"], WIN * b + w + 1)
                    V.scalar_tensor_tensor(zd[:, w], zd[:, w].bitcast(f32), d_low[:], zdbank[w][:], ALU.mult, ALU.add).then_inc(s["zd_done"], 1)

                def down(b, t, tiles):
                    pass

                def down_tail(b, t):
                    dve.wait_ge(s["out_mm"], NT * b + t + 1)
                    dve.wait_ge(s["x1_kept"], b + 1)
                    V.tensor_tensor(xres[:, t], xres[:, t], obank[t][:], ALU.add).then_inc(s["out_added"], 1)

            def normalise(b, t):
                dve.wait_ge(s["rstd2_done"], NT * b + t + 1)
                V.tensor_scalar(xn2[:, t], x[:, t], mv2[:, t, 0:1], rstd2[:, t:t + 1], ALU.subtract, ALU.mult).then_inc(s["xn2_done"], 1)

            xm_ = xm
            program(dve, Stages)

        @block.gpsimd
        def _(pool):
            G = nc.gpsimd

            class Stages:
                def split_windows():
                    pass

                def qk(b):
                    pass

                def stats(b):
                    pool.wait_ge(s["consts_set"], 1)
                    pool.wait_ge(s["mv1_done"], b + 1)
                    G.tensor_tensor(ve1[:], mv1[:, :, 1], eps[:], ALU.add).then_inc(s["ve1_done"], 1)
                    pool.wait_ge(s["ve1_done"], b + 1)
                    G.tensor_tensor(rstd1[:], ve1[:], neghalf[:], ALU.pow).then_inc(s["rstd1_done"], 1)

                def energy(b, t):
                    pass

                def softmax(b):
                    pass

                def mean_shift(b):
                    pass

                def scale(b):
                    pass

                def residual(r):
                    pool.wait_ge(s["res_mul"], 2 * r + 2)
                    if r < 2 * CLS:
                        dst = gu_r[r // CLS][:, r % CLS]
                    else:
                        if r == 2 * CLS:
                            pool.wait_ge(s["du_done"], 1)
                        dst = d_r[:, r - 2 * CLS]
                    G.tensor_tensor(dst, prod2[:, r % 2, 0], prod2[:, r % 2, 1], ALU.add).then_inc(s["res_done"], 1)

                def prob_t(b, t):
                    pass

                def split_x(b):
                    pass

                def coefficients(n):
                    pass

                def jumps():
                    pass

                def xm(b, t):
                    pool.wait_ge(s["mv2_done"], NT * b + t + 1)
                    G.tensor_tensor(ve2[:, t:t + 1], mv2[:, t, 1:2], eps[:, t:t + 1], ALU.add).then_inc(s["ve2_done"], 1)
                    pool.wait_ge(s["ve2_done"], NT * b + t + 1)
                    G.tensor_tensor(rstd2[:, t:t + 1], ve2[:, t:t + 1], neghalf[:, t:t + 1], ALU.pow).then_inc(s["rstd2_done"], 1)

                def norm_t(b, t):
                    pass

                def project(b):
                    pool.wait_ge(s["res_done"], 2 * CLS + MT)
                    pool.wait_ge(s["x1_added"], NT * (b + 1))
                    pool.wait_ge(s["out_stored"], 16 * NT * b + 1)
                    G.tensor_tensor(xres[:], x[:], ones[:].broadcast_to([P, NT, HID]), ALU.mult).then_inc(s["x1_kept"], 1)

                def gate_up(b, m):
                    pool.wait_ge(s["ih_done"], MT * b + m + 1)
                    if m >= 2:
                        pool.wait_ge(s["zd_mm"], MT * b + m - 1)
                    G.tensor_tensor(il[:, m % 2], inter[:, m % 3], ih[:, m].bitcast(f32), ALU.subtract).then_inc(s["il_done"], 1)

                def down_basis(b, m):
                    pass

                def down_split(b, w):
                    pass

                def down(b, t, tiles):
                    pass

                def down_tail(b, t):
                    pass

            program(pool, Stages)

        @block.tensor
        def _(pe):
            mm = nc.tensor.matmul

            class Stages:
                def split_windows():
                    pe.wait_ge(s["w_in"], 8 * 16)

                def qk(b):
                    pe.wait_ge(s["ctx_in"], 16 * (b + 1))
                    pe.wait_ge(s["xn2t_copied"], NT * b)
                    for n in range(2):
                        for c in range(CTX // P):
                            last = mm(abank[n][:], wqk[:, n, c], ctxT[:, c], start=c == 0, stop=c == CTX // P - 1)
                        last.then_inc(s["qk_mm"], 1)

                def stats(b):
                    pass

                def energy(b, t):
                    if t == 0:
                        pe.wait_ge(s["qk_done"], 2 * b + 2)
                    if t >= 2:
                        pe.wait_ge(s["exp_done"], NT * b + t - 1)
                    mm(abank[t % 2][:], qk_[:, 0, t * P:(t + 1) * P], qk_[:, 1], start=True, stop=True).then_inc(s["energy_mm"], 1)

                def softmax(b):
                    pass

                def mean_shift(b):
                    pass

                def scale(b):
                    pass

                def residual(r):
                    if r >= 2:
                        pe.wait_ge(s["res_mul"], 2 * (r - 1))
                    if r == 0:
                        pe.wait_ge(s["win_split"], 1)
                    if r == 2 * CLS:
                        pe.wait_ge(s["jump_split"], 2)
                    for k in range(2):
                        dst = bank[2 * (r % 2) + k][:]
                        if r < 2 * CLS:
                            p, c = HALF * (r // CLS), slice(r % CLS * HID, (r % CLS + 1) * HID)
                            last = mm(dst, pick[p:p + HALF, r % CLS, k], win_hl[p:p + HALF, c], start=True, stop=True)
                        else:
                            last = mm(dst, spread[:, r - 2 * CLS], jump[k], start=True, stop=True)
                    last.then_inc(s["res_mm"], 1)

                def prob_t(b, t):
                    if t == 0:
                        pe.wait_ge(s["prob_done"], NT * (b + 1))
                    if t >= 2:
                        pe.wait_ge(s["pl_done"], NT * b + t - 1)
                    for m in range(NT):
                        last = nc.tensor.transpose(abank[t % 2][:, m * P:(m + 1) * P], prob[:, m, t * P:(t + 1) * P], ident[:])
                    last.then_inc(s["pT_mm"], 1)

                def split_x(b):
                    pass

                def coefficients(n):
                    pe.wait_ge(s["stack_done"], n + 1)
                    for g in range(4):
                        if 4 * n + g >= 2:
                            pe.wait_ge(s["stack_out"], 4 * n + g - 1)
                        for k in range(4):
                            if n < 2:
                                src = stack[:, (4 * g + k) * G_K:(4 * g + k + 1) * G_K]
                            else:
                                src = stack[:, (WIN * k + g) * P:(WIN * k + g + 1) * P]
                            last = nc.tensor.transpose(bank[4 + g % 2][0:src.shape[1], k * P:(k + 1) * P], src, ident[:])
                        last.then_inc(s["stack_mm"], 1)

                def jumps():
                    pass

                def xm(b, t):
                    if t == 0:
                        pe.wait_ge(s["xsplit_done"], b + 1)
                        pe.wait_ge(s["pl_done"], NT * (b + 1))
                    if t >= 2:
                        pe.wait_ge(s["xm_scaled"], NT * b + t - 1)
                    c = slice(t * P, (t + 1) * P)
                    for n in range(NT):
                        mm(abank[t % 2][:], xh[:, n, c], ph[:, n], start=n == 0, stop=False)
                        mm(abank[t % 2][:], xh[:, n, c], pl[:, n], start=False, stop=False)
                        last = mm(abank[t % 2][:], xl[:, n, c], ph[:, n], start=False, stop=n == NT - 1)
                    last.then_inc(s["xm_mm"], 1)

                def norm_t(b, t):
                    if t == 0:
                        pe.wait_ge(s["xn2_done"], NT * (b + 1))
                        pe.wait_ge(s["xm_scaled"], NT * (b + 1))
                    if t >= 2:
                        pe.wait_ge(s["xn2t_copied"], NT * b + t - 1)
                    for l in range(NT):
                        last = nc.tensor.transpose(abank[t % 2][:, l * P:(l + 1) * P], xn2[:, l, t * P:(t + 1) * P], ident[:])
                    last.then_inc(s["xn2T_mm"], 1)

                def project(b):
                    pe.wait_ge(s["xn2t_copied"], NT * (b + 1))
                    pe.wait_ge(s["stack_out"], 12)
                    for a in range(CLS):
                        last = mm(zgbank[0:G_K, :], g_basis[:, a], xn2T[:, a], start=a == 0, stop=a == CLS - 1)
                    last.then_inc(s["zg_mm"], 1)

                def gate_up(b, m):
                    w, a = m // CLS, m % CLS
                    if m == 0:
                        pe.wait_ge(s["zg_done"], b + 1)
                        pe.wait_ge(s["xn2r_done"], NT * (b + 1))
                        pe.wait_ge(s["res_done"], 2 * CLS + MT)
                    for n, (dst, read) in enumerate(((gbank, "silu_done"), (ubank, "mult_done"))):
                        if m >= 2:
                            pe.wait_ge(s[read], MT * b + m - 1)
                        mm(dst[m % 2][:], gu_r[n][:, a, w * P:(w + 1) * P], xn2r[:, a], start=True, stop=False)
                    for n, (dst, done) in enumerate(((gbank, "g_mm"), (ubank, "u_mm"))):
                        mm(dst[m % 2][:], gu_v[n][:, m], zg, start=False, stop=True).then_inc(s[done], 1)

                def down_basis(b, m):
                    w, a = m // CLS, m % CLS
                    if a == 0 and w >= 2:
                        pe.wait_ge(s["zd_done"], WIN * b + w - 1)
                    if m == 0:
                        pe.wait_ge(s["du_done"], 1)
                    pe.wait_ge(s["il_done"], MT * b + m + 1)
                    u = d_u[:, m].rearrange("p k f -> p (k f)")
                    mm(zdbank[w][:], u, ih[:, m], start=a == 0, stop=False)
                    mm(zdbank[w][:], u, il[:, m % 2], start=False, stop=a == CLS - 1).then_inc(s["zd_mm"], 1)

                def down_split(b, w):
                    pass

                def down(b, t, tiles):
                    if t == 0:
                        if tiles[0] == 0:
                            pe.wait_ge(s["silu_done"], MT * b + MT - 1)
                        pe.wait_ge(s["ih_done"], MT * b + tiles[-1] + 1)
                    if t == 1:
                        pe.wait_ge(s["mult_done"], MT * (b + 1))
                    for m in tiles:
                        mm(obank[t][:], ih[:, m, t * P:(t + 1) * P], d_r[:, m], start=m == 0, stop=False)

                def down_tail(b, t):
                    if t == 0:
                        pe.wait_ge(s["zd_done"], WIN * (b + 1))
                    for w in range(WIN):
                        last = mm(obank[t][:], zd[:, w, t * P:(t + 1) * P], d_v[:, w], start=False, stop=w == WIN - 1)
                    last.then_inc(s["out_mm"], 1)

            qk_ = qk
            program(pe, Stages)


def kernel(x, ctx_1024, L0_xattn_Wq, L0_xattn_bq, L0_xattn_Wk, L0_xattn_bk, L0_ffn_gate_cp, L0_ffn_up_cp, L0_ffn_down_cp):
    import concourse.bacc as bacc
    from concourse.bass_utils import run_bass_kernel_spmd

    c, at, hidden, _ = constants()
    x, ctx_1024, wq, bq, wk, bk, gate, up, down = (np.asarray(a) for a in (
        x, ctx_1024, L0_xattn_Wq, L0_xattn_bq, L0_xattn_Wk, L0_xattn_bk, L0_ffn_gate_cp, L0_ffn_up_cp, L0_ffn_down_cp))
    x, context = x[:, :, hidden], ctx_1024[:, hidden]

    def tiled(a):
        return a.reshape(*a.shape[:-2], -1, P, a.shape[-1]).swapaxes(-3, -2)

    arrays = dict(
        c, x=tiled(x), xT=tiled(x.swapaxes(1, 2)), ctxT=tiled(context.swapaxes(1, 2)),
        wqT=tiled(wq.T), wkT=tiled(wk.T), bq=bq.reshape(DK, 1), bk=bk.reshape(DK, 1),
        g_node=gate[at["g_node"]].reshape(P, -1), u_node=up[at["g_node"]].reshape(P, -1),
        g_win=gate[at["g_win"]], u_win=up[at["g_win"]],
        d_node=down[at["d_node"]].reshape(P, -1), d_knot=down[at["d_knot"]].reshape(P, -1))
    arrays = {f"in_{k}": np.ascontiguousarray(v) for k, v in arrays.items()}
    nc = bacc.Bacc("TRN2", target_bir_lowering=False, num_devices=1)
    d = {k[3:]: nc.dram_tensor(k, v.shape, mybir.dt.from_np(v.dtype), kind="ExternalInput").ap() for k, v in arrays.items()}
    out = nc.dram_tensor("out", (B, NT, P, HID), mybir.dt.float32, kind="ExternalOutput").ap()
    xattn_spline_ffn_kernel(nc, d, out)
    got = run_bass_kernel_spmd(nc, [arrays], core_ids=[0]).results[0]["out"]
    back = np.argsort(hidden)
    return np.ascontiguousarray(got.reshape(B, TOK, HID)[:, :, back])
```

```python
import numpy as np
import concourse.bass as bass
from concourse import mybir
from contextlib import ExitStack

BF16 = mybir.dt.np(mybir.dt.bfloat16)
B, TOK, HID, CTX, DK, INTER = 4, 512, 512, 256, 128, 2048
NCTRL = int(INTER * HID / 128.9)
STEP = (NCTRL - 1) / (INTER * HID - 1)
PERIOD = 1 / STEP
P = 128
NT = HID // P
CLS = 4
MT = INTER // P
G_NODES = 4 * CLS + 1
G_FN = 2 * G_NODES
G_K = 3 * G_FN
WIN = 4
D_NODES = 16
D_FN = 2 * D_NODES
D_CELLS = WIN * (D_NODES - 1)
LAG = 3
CHUNKS = 3 * 4
HALF = 64
WIDTH = PERIOD / 4
S2, S3 = 256.0, 2048.0
EPS = 1e-5


def hermite(u):
    return 2 * u**3 - 3 * u**2 + 1, u**3 - 2 * u**2 + u, 3 * u**2 - 2 * u**3, u**3 - u**2


def basis_at(pos, nodes):
    c = np.clip(np.searchsorted(nodes, pos, side="right") - 1, 0, len(nodes) - 2)
    width = nodes[c + 1] - nodes[c]
    out = np.zeros((len(pos), 2 * len(nodes)))
    for k, h in enumerate(hermite((pos - nodes[c]) / width)):
        out[np.arange(len(pos)), 2 * c + k] = h * (width / WIDTH if k % 2 else 1)
    return out, c


def node_taps(t):
    k = np.floor(t).astype(np.int64)
    f = t - k
    value = 0.5 * np.stack([-f + 2 * f**2 - f**3, 2 - 5 * f**2 + 3 * f**3, f + 4 * f**2 - 3 * f**3, f**3 - f**2], -1)
    slope = 0.5 * np.stack([4 * f - 1 - 3 * f**2, 9 * f**2 - 10 * f, 1 + 8 * f - 9 * f**2, 3 * f**2 - 2 * f], -1)
    return control(k[..., None] + np.arange(-1, 3)), np.stack([value, slope * (WIDTH * STEP)], -2)


def control(k):
    return np.clip(k, 0, NCTRL - 1)


def cell_residual(pos, left, right, knot):
    inside = (knot > left) & (knot < right)
    knot = np.where(inside, knot, right)
    width = right - left
    _, _, value, slope = hermite((pos - left) / width)
    x, e = np.maximum(pos - knot, 0) * STEP, (right - knot) * STEP
    r2 = x**2 - (value * e**2 + slope * 2 * e * width * STEP)
    r3 = x**3 - (value * e**3 + slope * 3 * e**2 * width * STEP)
    return np.where(inside, r2, 0) * S2, np.where(inside, r3, 0) * S3


def gate_layout():
    start = np.arange(INTER) * HID * STEP
    first = PERIOD * (1 - (start - np.floor(start)))
    for offset in np.arange(-4.7, 0, 0.1):
        turn = (first - offset) % PERIOD
        order = np.sort(turn)
        edge = np.array([0] + [order[a * HID - 1:a * HID + 1].mean() for a in range(1, CLS)])
        nodes = np.append((offset + np.arange(4)[:, None] * PERIOD + edge).ravel(), offset + 4 * PERIOD)
        cell = np.searchsorted(nodes, np.arange(HID), side="right") - 1
        if nodes[-1] >= HID - 1 and (np.bincount(cell % CLS) == P).all():
            break
    else:
        raise ValueError("no layout with equal classes")
    cls = np.searchsorted(edge, turn, side="right") - 1
    hidden = np.argsort(cell % CLS, kind="stable")
    rows = np.stack([np.flatnonzero(cls == a) for a in range(CLS)]).reshape(CLS, WIN, P)
    knot = np.rint(start + (offset + turn) * STEP).astype(np.int64)
    return nodes, cell, hidden, rows, knot, start


def constants():
    nodes, cell, hidden, rows, knot, start = gate_layout()
    c, at = {}, {}
    tiles = rows.transpose(1, 0, 2).reshape(MT, P)
    idx, coef = node_taps(start[tiles.T][:, :, None] + nodes * STEP)
    at["g_node"] = idx.reshape(P, MT * G_NODES, 4)
    c["g_coef"] = coef.reshape(P, MT * G_NODES * 8).astype(np.float32)
    u = basis_at(hidden.astype(float), nodes)[0].reshape(CLS, P, G_FN)
    c["g_basis"] = np.tile(u.transpose(1, 0, 2)[:, :, None], (1, 1, 3, 1)).reshape(P, CLS * G_K).astype(np.float32)
    lo = (np.arange(G_K) // G_FN) == 1
    c["g_low"] = np.where(lo, -1.0, 0.0).reshape(G_K, 1).astype(np.float32)
    byclass = rows.reshape(INTER)
    win = np.zeros((32, INTER), np.int64)
    win[:8] = control(knot[byclass] + np.arange(-2, 6)[:, None])
    at["g_win"] = win
    jump = {2: np.array([0.5, -1, 0, 1, -0.5]), 3: np.array([0.5, -2, 3, -2, 0.5])}
    pick = np.zeros((32, CLS, 2, P))
    r2, r3 = np.zeros((P, INTER)), np.zeros((P, INTER))
    for a in range(CLS):
        h = hidden[a * P:(a + 1) * P]
        for n in range(4):
            pick[n:n + 5, a, 0, cell[h] // CLS == n] = jump[2][:, None] / S2
            pick[n:n + 5, a, 1, cell[h] // CLS == n] = jump[3][:, None] / S3
        i = rows[a].ravel()
        place = ((knot[i] + (cell[h] // CLS)[:, None]) - start[i]) * PERIOD
        left, right = nodes[cell[h]][:, None], nodes[cell[h] + 1][:, None]
        r2[:, a * HID:(a + 1) * HID], r3[:, a * HID:(a + 1) * HID] = cell_residual(h[:, None], left, right, place)
    c["g_pick"] = np.tile(pick.reshape(32, CLS * 2 * P), (4, 1)).astype(BF16)
    c["g_winlow"] = np.where(np.arange(P) // 32 % 2 == 1, -1.0, 0.0).reshape(P, 1).astype(np.float32)
    c["g_r2"], c["g_r3"] = r2.astype(np.float16), r3.astype(np.float16)
    window = tiles.reshape(WIN, CLS * P)
    dn = np.stack([np.linspace(w.min(), w.max(), D_NODES) for w in window])
    t = hidden.reshape(NT, P).T[:, None, :, None] * (INTER * STEP) + dn[:, None] * STEP
    idx, coef = node_taps(t)
    at["d_node"] = idx.reshape(P, NT * WIN * D_NODES, 4)
    c["d_coef"] = coef.reshape(P, NT * WIN * D_NODES * 8).astype(np.float32)
    basis, spread = np.zeros((P, MT, D_FN)), np.zeros((HALF, MT, P))
    left, right = dn[:, :-1].ravel(), dn[:, 1:].ravel()
    row0 = hidden * (INTER * STEP)
    kd = np.floor(row0 + right[:, None] * STEP).astype(np.int64)
    at["d_knot"] = np.zeros((2, HALF, 5, HID), np.int64)
    at["d_knot"][:, :D_CELLS] = control(kd[:, None] + np.arange(-2, 3)[:, None])
    place = (kd - row0) * PERIOD
    r2, r3 = np.zeros((P, MT, HID)), np.zeros((P, MT, HID))
    for m in range(MT):
        basis[:, m], k = basis_at(tiles[m].astype(float), dn[m // CLS])
        k = k + (m // CLS) * (D_NODES - 1)
        spread[k, m, np.arange(P)] = 0.5 / S2
        r2[:, m], r3[:, m] = cell_residual(tiles[m][:, None], left[k][:, None], right[k][:, None], place[k])
    c["d_basis"] = basis.reshape(P, MT * D_FN).astype(np.float32)
    c["d_spread"] = np.tile(spread.reshape(HALF, INTER), (2, 1)).astype(BF16)
    c["d_r2"], c["d_r3"] = (r.reshape(P, 4, 4 * HID).transpose(1, 0, 2).astype(np.float16) for r in (r2, r3))
    c["d_low"] = np.where(np.arange(P) // D_FN == 1, -1.0, 0.0).reshape(P, 1).astype(np.float32)
    c["ident"] = np.eye(P, dtype=np.float32)
    return c, at, hidden, tiles


def xattn_spline_ffn_kernel(nc: bass.Bass, d, out: bass.AP):
    f32, f32r, bf16, fp16 = mybir.dt.float32, mybir.dt.float32r, mybir.dt.bfloat16, mybir.dt.float16
    ALU, ACT, AX = mybir.AluOpType, mybir.ActivationFunctionType, mybir.AxisListType

    ctx = ExitStack()
    with ctx:
        def sb(name, shape, dt, stack=ctx):
            return stack.enter_context(nc.sbuf_tensor(name, shape, dt))

        def sem(name):
            return ctx.enter_context(nc.semaphore(name))

        wqk = sb("wqk", [P, 2, CTX // P, DK], f32)
        bqk = sb("bqk", [DK, 2], f32)
        ident = sb("ident", [P, P], f32)
        g_basis = sb("g_basis", [P, CLS, G_K], f32)
        g_low = sb("g_low", [G_K, 1], f32)
        d_low = sb("d_low", [P, 1], f32)
        g_winlow = sb("g_winlow", [P, 1], f32)
        neghalf = sb("neghalf", [P, NT], f32)
        eps = sb("eps", [P, NT], f32)
        ones = sb("ones", [P, 1, 1], f32)
        gu_r = [sb(f"{n}_r", [P, CLS, WIN * P], f32r) for n in ("gate", "up")]
        gu_v = [sb(f"{n}_v", [G_K, MT, P], f32r) for n in ("gate", "up")]
        d_v = sb("d_v", [P, WIN, HID], f32r)
        d_u = sb("d_u", [P, MT, 4, D_FN], f32r)
        ctxT = sb("ctxT", [P, CTX // P, TOK], f32)
        qk = sb("qk", [P, 2, TOK], f32)
        x = sb("x", [P, NT, HID], f32)
        xT = sb("xT", [P, NT, TOK], f32)
        xh = sb("xh", [P, NT, TOK], f32r)
        xl = sb("xl", [P, NT, TOK], f32r)
        prob = sb("prob", [P, NT, TOK], f32)
        ph = sb("ph", [P, NT, TOK], f32r)
        pl = sb("pl", [P, NT, TOK], f32r)
        nmax = sb("nmax", [P, NT], f32)
        rsum = sb("rsum", [P, NT], f32)
        rinv = sb("rinv", [P, NT], f32)
        bst1, bst2 = sb("bst1", [P, NT, 6], f32), sb("bst2", [P, NT, 6], f32)
        mv1, mv2 = sb("mv1", [P, NT, 2], f32), sb("mv2", [P, NT, 2], f32)
        ve1, ve2 = sb("ve1", [P, NT], f32), sb("ve2", [P, NT], f32)
        rstd1, rstd2 = sb("rstd1", [P, NT], f32), sb("rstd2", [P, NT], f32)
        nmr1 = sb("nmr1", [P, NT], f32)
        xn2, xn2T, xn2r, xm = xT, prob, xh, qk

        prep = ExitStack()
        coef = sb("coef", [P, MT, G_NODES, 2, 4], f32, prep)
        gate_pt, up_pt = (sb(n, [P, MT, G_NODES, 1, 4], f32, prep) for n in ("gate_pt", "up_pt"))
        d_coef = sb("d_coef", [P, WIN, NT * D_NODES, 2, 4], f32, prep)
        down_pt = sb("down_pt", [P, WIN, NT * D_NODES, 1, 4], f32, prep)
        basis_f = sb("basis_f", [P, MT, D_FN], f32, prep)
        sb("pad", [P, MT * HID - MT * G_NODES * 16 - WIN * NT * D_NODES * 12 - MT * D_FN], f32, prep)
        prod = sb("prod", [P, 2, CLS * G_NODES * 8], f32, prep)
        fval = sb("fval", [P, 2, CLS * G_FN], f32, prep)
        stack = sb("stack", [P, 2, NT * P], f32, prep)
        prod2 = sb("prod2", [P, 2, 2, HID], f32, prep)
        work = sb("work", [P, 6144], f32, prep)
        pick = sb("pick", [P, CLS, 2, P], bf16, prep)
        knots = sb("knots", [P, 5, HID], f32, prep)
        spread = sb("spread", [P, MT, P], bf16, prep)
        prep.close()
        d_r = sb("d_r", [P, MT, HID], f32r)
        ih = sb("ih", [P, MT, TOK], f32r)
        xres = sb("xres", [P, NT, HID], f32)
        inter = sb("inter", [P, 3, TOK], f32)
        il = sb("il", [P, 2, TOK], f32r)
        zd = sb("zd", [P, WIN, TOK], f32r)
        zg = zd[0:G_K, WIN - 1, :]

        r2g, r3g = (work[:, n * 1024:(n + 1) * 1024].bitcast(fp16) for n in range(2))
        win = work[:, 2048:4096]
        win_h, win_hl = (work[:, 4096 + n * 1024:5120 + n * 1024].bitcast(bf16) for n in range(2))
        rd = [[work[:, s * 2048 + n * 1024:s * 2048 + (n + 1) * 1024].bitcast(fp16) for n in range(2)] for s in range(3)]
        ja, jb = (win[:, n * HID:(n + 1) * HID] for n in range(2))
        jump = [knots[:, 3 + n, 0:HID // 2].bitcast(bf16) for n in range(2)]

        def chunk(k):
            g, slot = k % 4, k % 2
            if k < 8:
                tiles, fn, copies, low = 4, G_FN, 3, 2
                cf, pt = coef[:, 4 * g:4 * g + 4].rearrange("p m n v t -> p (m n) v t"), (gate_pt, up_pt)[k // 4][:, 4 * g:4 * g + 4].rearrange("p m n v t -> p (m n) v t")
                dst = gu_v[k // 4][:, 4 * g:4 * g + 4].rearrange("p m i -> p (m i)")
            else:
                tiles, fn, copies, low = NT, D_FN, 4, 3
                cf, pt = d_coef[:, g], down_pt[:, g]
                dst = d_v[:, g]
            nodes = tiles * fn // 2
            pr = prod[:, slot, 0:nodes * 8]
            val = fval[:, slot, 0:tiles * fn]
            st = stack[:, slot, 0:tiles * copies * fn]
            return dict(nodes=nodes, low=low, coef=cf, points=pt.broadcast_to([P, nodes, 2, 4]), prod=pr, sums=val, dst=dst,
                        val=val.rearrange("p (m f) -> p m f", m=tiles), copies=copies, width=copies * fn,
                        stack=st, parts=st.rearrange("p (m k f) -> p m k f", m=tiles, k=copies))

        bank = [ctx.enter_context(nc.psum_tensor(f"bank{n}", [P, 512], f32)) for n in range(8)]
        gbank, ubank, obank = bank[0:2], bank[2:4], bank[0:4]
        zgbank, zdbank = bank[4], [bank[5], bank[4], bank[5], bank[4]]
        abank = bank[6:8]

        names = """wqk_in bqk_in ident_in basis_in ctx_in x_in xt_in win_in r_in node_in upnode_in dnode_in dbasis_in knot_in
            rd0_in rd1_in rd2_in out_stored
            consts_set win_hi win_split jump_sums jump_k2 jump_c jump_d jump_hi jump_split res_mm res_mul res_done
            tap_mul tap_sum stack_hi stack_done stack_mm stack_out du_hi du_done
            qk_mm qk_done energy_mm max_done exp_done rinv_done prob_done pT_mm ph_done pl_done
            stats1 mv1_done ve1_done rstd1_done nmr_done xh_done xsplit_done xm_mm xm_scaled x1_added
            stats2 mv2_done ve2_done rstd2_done xn2_done xn2T_mm xn2t_copied xn2r_done
            x1_kept zg_mm zg_hi zg_done g_mm u_mm silu_done mult_done ih_done il_done zd_mm zd_hi zd_done
            out_mm out_added"""
        s = {n: sem(n) for n in names.split()}

        def attention_only(st):
            st.constants()
            for a in range(4):
                st.split_windows(a)
            st.qk(0)
            st.tap_products(0)
            st.softmax(0, 0)
            st.energy(0, 0)
            st.softmax(0, 1)
            st.residual(0)
            st.softmax(0, 2)
            st.energy(0, 1)
            st.spread(0)
            for t in range(2, 4):
                st.energy(0, t)
            st.softmax(0, 3)
            st.spread(1)
            st.tap_products(1)
            st.residual(1)
            st.scale(0)
            st.spread(2)
            st.prob_t(0, 0)
            st.tap_products(2)
            st.spread(3)
            st.tap_products(3)
            for k in range(2):
                st.tap_sums(k)
            st.stack_parts(0)
            st.residual(2)
            st.spread(4)
            st.tap_sums(2)
            st.residual(3)
            st.prob_t(0, 1)
            for t in range(2):
                st.split_prob(0, t)
            st.stack_parts(1)
            st.spread(5)
            st.residual(4)
            st.spread(6)
            st.tap_sums(3)
            st.prob_t(0, 2)
            st.tap_products(4)
            st.jump_inputs()
            st.stack_parts(2)
            for r in range(5, 7):
                st.residual(r)
            st.stack_parts(3)
            st.spread(7)
            st.tap_sums(4)
            st.stats(0)
            st.tap_products(5)
            st.prob_t(0, 3)
            st.split_prob(0, 2)
            st.tap_products(6)
            st.split_prob(0, 3)
            st.split_x(0)
            st.stack_parts(4)
            st.xm(0, 0)
            st.tap_products(7)
            st.mean_shift(0)
            st.xm(0, 1)
            st.residual(7)
            for k in range(8, 10):
                st.tap_products(k)
            st.tap_sums(5)
            st.jumps()
            st.spread(8)
            st.add_xm(0, 0)
            st.tap_sums(6)
            st.stack_parts(5)
            st.tap_sums(7)
            st.stack_parts(6)
            st.spread(9)
            st.residual(8)
            st.spread(10)
            st.xm(0, 2)
            st.tap_sums(8)
            st.tap_products(10)
            st.spread(11)
            st.residual(9)
            st.add_xm(0, 1)
            st.xm(0, 3)
            st.residual(10)
            for t in range(2, 4):
                st.add_xm(0, t)
            st.spread(12)
            st.stack_parts(7)
            st.spread(13)
            for r in range(11, 13):
                st.residual(r)
            st.tap_products(11)
            st.tap_sums(9)
            st.stack_parts(8)
            st.spread(14)
            st.tap_sums(10)
            st.stack_parts(9)
            for r in range(13, 15):
                st.residual(r)
            st.tap_sums(11)
            st.residual(15)
            st.spread(15)
            st.residual(16)
            st.spread(16)
            st.cast_t(0, 0)
            st.norm_t(0, 0)
            st.spread(17)
            for k in range(10, 12):
                st.stack_parts(k)
            for r in range(17, 20):
                st.residual(r)
            for r in range(18, 21):
                st.spread(r)
            for r in range(20, 22):
                st.residual(r)
            st.cast_t(0, 1)
            st.down_factors()
            st.norm_t(0, 1)
            st.cast_t(0, 2)
            st.spread(21)
            for t in range(2, 4):
                st.norm_t(0, t)
            st.cast_t(0, 3)
            st.spread(22)
            st.residual(22)
            st.spread(23)
            st.residual(23)

        def ffn(st, b, a=None):
            st.project(b)
            for m in range(2):
                st.activate(b, m)
            if a is not None:
                st.qk(a)
            st.gate_up(b, 0)
            st.activate(b, 2)
            for m in range(1, 3):
                st.gate_up(b, m)
            st.activate(b, 3)
            st.gate_up(b, 3)
            st.activate(b, 4)
            st.down_basis(b, 0)
            st.gate_up(b, 4)
            st.down_basis(b, 1)
            st.activate(b, 5)
            st.gate_up(b, 5)
            st.activate(b, 6)
            st.down_basis(b, 2)
            st.down_split(b, 0)
            st.activate(b, 7)
            st.gate_up(b, 6)
            st.down_basis(b, 3)
            st.gate_up(b, 7)
            st.down_basis(b, 4)
            st.gate_up(b, 8)
            st.down_basis(b, 5)
            for m in range(8, 10):
                st.activate(b, m)
            st.gate_up(b, 9)
            st.activate(b, 10)
            st.down_basis(b, 6)
            st.gate_up(b, 10)
            st.down_basis(b, 7)
            st.gate_up(b, 11)
            st.down_basis(b, 8)
            st.down_split(b, 1)
            for m in range(11, 13):
                st.activate(b, m)
            st.gate_up(b, 12)
            for m in range(13, 15):
                st.activate(b, m)
            st.down_basis(b, 9)
            st.gate_up(b, 13)
            st.down_split(b, 2)
            st.down_basis(b, 10)
            st.gate_up(b, 14)
            st.down_basis(b, 11)
            st.gate_up(b, 15)
            st.activate(b, 15)
            st.down_basis(b, 12)
            if a is not None:
                st.split_x(a)
                st.softmax(a, 0)
                st.energy(a, 0)
            st.down_basis(b, 13)
            if a is not None:
                st.softmax(a, 1)
                st.energy(a, 1)
            st.down(b, 0, range(MT - LAG))
            for m in range(14, 16):
                st.down_basis(b, m)
            if a is not None:
                st.energy(a, 2)
            st.down_split(b, 3)
            if a is not None:
                st.energy(a, 3)
                st.softmax(a, 2)
            st.down(b, 0, range(MT - LAG, MT))
            if a is not None:
                st.softmax(a, 3)
            st.down(b, 1, range(MT))
            if a is not None:
                st.scale(a)
                st.split_prob(a, 0)
                for t in range(2):
                    st.prob_t(a, t)
                st.split_prob(a, 1)
            for t in range(2):
                st.down_tail(b, t)
            if a is not None:
                st.prob_t(a, 2)
                st.split_prob(a, 2)
                st.prob_t(a, 3)
                st.split_prob(a, 3)
                for t in range(3):
                    st.xm(a, t)
                st.stats(a)
                st.mean_shift(a)
                for t in range(2):
                    st.add_xm(a, t)
                st.xm(a, 3)
                for t in range(2, 4):
                    st.add_xm(a, t)
                st.cast_t(a, 0)
            st.down(b, 2, range(MT))
            st.down_tail(b, 2)
            if a is not None:
                st.cast_t(a, 1)
                for t in range(2):
                    st.norm_t(a, t)
                st.cast_t(a, 2)
            st.down(b, 3, range(MT))
            if a is not None:
                for t in range(2, 4):
                    st.norm_t(a, t)
                st.cast_t(a, 3)
            st.down_tail(b, 3)

        def program(eng, st):
            attention_only(st)
            with eng.Fori(0, B - 1) as b:
                ffn(st, b, b + 1)
            ffn(st, B - 1)

        block = ctx.enter_context(nc.Block())

        @block.sync
        def _(sp):
            def load(dst, name, signal):
                sp.dma_start(dst, d[name]).then_inc(s[signal], 16)

            load(wqk[:, 1], "wkT", "wqk_in")
            load(wqk[:, 0], "wqT", "wqk_in")
            sp.dma_start(ctxT[:], d["ctxT"][0]).then_inc(s["ctx_in"], 16)
            for n, name in enumerate(("g_win", "g_win", "u_win", "u_win")):
                load(win[32 * n:32 * n + 32, :], name, "win_in")
            load(g_winlow[:], "g_winlow", "win_in")
            load(bqk[:, 0:1], "bq", "bqk_in")
            load(pick[:].rearrange("p a k n -> p (a k n)"), "g_pick", "win_in")
            load(bqk[:, 1:2], "bk", "bqk_in")
            load(r2g, "g_r2", "r_in")
            load(gate_pt[:].rearrange("p m n v t -> p (m n v t)"), "g_node", "node_in")
            load(r3g, "g_r3", "r_in")
            load(coef[:].rearrange("p m n v t -> p (m n v t)"), "g_coef", "node_in")
            load(basis_f[:].rearrange("p m n -> p (m n)"), "d_basis", "dbasis_in")
            load(d_coef[:].rearrange("p m n v t -> p (m n v t)"), "d_coef", "dnode_in")
            load(g_low[:], "g_low", "basis_in")
            load(ident[:], "ident", "ident_in")
            load(knots[:].rearrange("p w n -> p (w n)"), "d_knot", "knot_in")
            load(spread[:].rearrange("p m n -> p (m n)"), "d_spread", "knot_in")
            load(up_pt[:].rearrange("p m n v t -> p (m n v t)"), "u_node", "upnode_in")
            sp.dma_start(x[:], d["x"][0]).then_inc(s["x_in"], 16)
            sp.dma_start(xT[:], d["xT"][0]).then_inc(s["xt_in"], 16)
            load(g_basis[:].rearrange("p a n -> p (a n)"), "g_basis", "basis_in")
            load(down_pt[:].rearrange("p m n v t -> p (m n v t)"), "d_node", "dnode_in")
            load(d_low[:], "d_low", "basis_in")

            def quarter(slot, q):
                for n in range(2):
                    sp.dma_start(rd[slot][n], d[f"d_r{n + 2}"][q]).then_inc(s[f"rd{slot}_in"], 16)

            sp.wait_ge(s["res_mul"], 4 * CLS)
            quarter(0, 0)
            quarter(2, 2)
            sp.wait_ge(s["jump_split"], 2)
            quarter(1, 1)
            sp.wait_ge(s["res_mul"], 2 * (2 * CLS + 4))
            quarter(0, 3)

            def store(b, t):
                sp.wait_ge(s["out_added"], NT * b + t + 1)
                sp.dma_start(out[bass.ds(b, 1), t].rearrange("a p n -> (a p) n"), xres[:, t]).then_inc(s["out_stored"], 16)

            def fetch(src, b):
                return d[src][bass.ds(b, 1)].rearrange("a p t n -> (a p) t n")

            def batch(b, more):
                sp.wait_ge(s["xn2_done"], NT * (b + 1))
                sp.wait_ge(s["x1_kept"], b + 1)
                sp.dma_start(x[:], fetch("x", b + 1)).then_inc(s["x_in"], 16)
                sp.wait_ge(s["xn2T_mm"], NT * (b + 1))
                sp.dma_start(xT[:], fetch("xT", b + 1)).then_inc(s["xt_in"], 16)
                if more:
                    sp.wait_ge(s["qk_mm"], 2 * b + 4)
                    sp.dma_start(ctxT[:], fetch("ctxT", b + 2)).then_inc(s["ctx_in"], 16)
                for t in range(NT):
                    store(b, t)

            sp.wait_ge(s["qk_mm"], 2)
            sp.dma_start(ctxT[:], d["ctxT"][1]).then_inc(s["ctx_in"], 16)
            with sp.Fori(0, B - 2) as b:
                batch(b, True)
            batch(B - 2, False)
            for t in range(NT):
                store(B - 1, t)
            sp.wait_ge(s["out_stored"], 16 * NT * B + 1)

        @block.scalar
        def _(act):
            class Stages:
                def constants():
                    pass

                def split_windows(a):
                    c = slice(a * HID, (a + 1) * HID)
                    act.wait_ge(s["win_in"], 6 * 16)
                    nc.scalar.activation(win_h[:, c], win[:, c], ACT.Copy).then_inc(s["win_hi"], 1)

                def qk(b):
                    for n in range(2):
                        act.wait_ge(s["qk_mm"], 2 * b + n + 1)
                        if n == 0:
                            act.wait_ge(s["bqk_in"], 2 * 16)
                            if not (isinstance(b, int) and b == 0):
                                act.wait_ge(s["x1_added"], NT * b)
                        nc.scalar.activation(qk_[:, n], abank[n][:], ACT.Identity, bias=bqk[:, n:n + 1]).then_inc(s["qk_done"], 1)

                def stats(b):
                    pass

                def energy(b, t):
                    pass

                def softmax(b, t):
                    act.wait_ge(s["max_done"], NT * b + t + 1)
                    if t == 0 and not (isinstance(b, int) and b == 0):
                        act.wait_ge(s["zg_mm"], b)
                    nc.scalar.activation(prob[:, t], abank[t % 2][:], ACT.Exp, bias=nmax[:, t:t + 1],
                                         accum_out=rsum[:, t:t + 1]).then_inc(s["exp_done"], 1)

                def mean_shift(b):
                    pass

                def scale(b):
                    pass

                def spread(r):
                    pass

                def residual(r):
                    pass

                def prob_t(b, t):
                    pass

                def split_prob(b, t):
                    act.wait_ge(s["pT_mm"], NT * b + t + 1)
                    nc.scalar.activation(ph[:, t], abank[t % 2][:], ACT.Copy).then_inc(s["ph_done"], 1)

                def split_x(b):
                    act.wait_ge(s["xt_in"], 16 * (b + 1))
                    if not (isinstance(b, int) and b == 0):
                        act.wait_ge(s["u_mm"], MT * b)
                    nc.scalar.activation(xh[:], xT[:], ACT.Copy).then_inc(s["xh_done"], 1)

                def tap_products(k):
                    pass

                def tap_sums(k):
                    c = chunk(k)
                    act.wait_ge(s["tap_sum"], k + 1)
                    if k >= 2:
                        act.wait_ge(s["stack_mm"], k - 1)
                    for n in range(c["low"]):
                        last = nc.scalar.activation(c["parts"][:, :, n].bitcast(f32r), c["val"], ACT.Copy)
                    last.then_inc(s["stack_hi"], 1)

                def stack_parts(k):
                    dst = chunk(k)["dst"]
                    act.wait_ge(s["stack_mm"], k + 1)
                    nc.scalar.activation(dst, bank[4 + k % 2][0:dst.shape[0], :], ACT.Copy).then_inc(s["stack_out"], 1)

                def jump_inputs():
                    act.wait_ge(s["knot_in"], 32)
                    nc.scalar.activation(knots[:, 2], knots[:, 2], ACT.Copy, scale=0.75).then_inc(s["jump_k2"], 1)

                def jumps():
                    for k in range(2):
                        act.wait_ge(s["jump_d"], k + 1)
                        nc.scalar.activation(jump[k], (ja, jb)[k], ACT.Copy).then_inc(s["jump_hi"], 1)

                def down_factors():
                    act.wait_ge(s["dbasis_in"], 16)
                    for k in (0, 1, 3):
                        last = nc.scalar.activation(d_u[:, :, k], basis_f[:], ACT.Copy)
                    last.then_inc(s["du_hi"], 1)

                def xm(b, t):
                    pass

                def add_xm(b, t):
                    act.wait_ge(s["xm_mm"], NT * b + t + 1)
                    if t == 0:
                        act.wait_ge(s["nmr_done"], b + 1)
                    if t >= 2:
                        act.wait_ge(s["x1_added"], NT * b + t - 1)
                    nc.scalar.activation(xm_[:, t % 2], abank[t % 2][:], ACT.Identity, bias=nmr1[:, t:t + 1],
                                         scale=rstd1[:, t:t + 1]).then_inc(s["xm_scaled"], 1)

                def cast_t(b, t):
                    act.wait_ge(s["xn2T_mm"], NT * b + t + 1)
                    nc.scalar.activation(xn2T[:, t], abank[t % 2][:], ACT.Copy).then_inc(s["xn2t_copied"], 1)

                def norm_t(b, t):
                    pass

                def project(b):
                    act.wait_ge(s["zg_mm"], b + 1)
                    if isinstance(b, int) and b == 0 or not isinstance(b, int):
                        act.wait_ge(s["res_done"], 2 * CLS + MT)
                    nc.scalar.activation(zg, zgbank[0:G_K, :], ACT.Copy).then_inc(s["zg_hi"], 1)

                def gate_up(b, m):
                    pass

                def activate(b, m):
                    act.wait_ge(s["g_mm"], MT * b + m + 1)
                    if m >= 3:
                        act.wait_ge(s["il_done"], MT * b + m - 2)
                    nc.scalar.activation(inter[:, m % 3], gbank[m % 2][:], ACT.Silu).then_inc(s["silu_done"], 1)

                def down_basis(b, m):
                    pass

                def down_split(b, w):
                    act.wait_ge(s["zd_mm"], MT * b + CLS * (w + 1))
                    nc.scalar.activation(zd[:, w], zdbank[w][:], ACT.Copy).then_inc(s["zd_hi"], 1)

                def down(b, t, tiles):
                    pass

                def down_tail(b, t):
                    pass

            qk_, xm_ = qk, xm
            program(act, Stages)

        @block.vector
        def _(dve):
            V = nc.vector

            class Stages:
                def constants():
                    V.memset(eps[:], EPS)
                    V.memset(ones[:], 1.0).then_inc(s["out_stored"], 1)
                    V.memset(neghalf[:], -0.5).then_inc(s["consts_set"], 1)

                def split_windows(a):
                    c = slice(a * HID, (a + 1) * HID)
                    dve.wait_ge(s["win_hi"], a + 1)
                    V.scalar_tensor_tensor(win_hl[:, c], win_h[:, c], g_winlow[:], win[:, c], ALU.mult, ALU.add).then_inc(s["win_split"], 1)

                def qk(b):
                    pass

                def stats(b):
                    dve.wait_ge(s["x_in"], 16 * (b + 1))
                    for t in range(NT):
                        last = V.bn_stats(bst1[:, t], x[:, t])
                    last.then_inc(s["stats1"], 1)
                    dve.wait_ge(s["consts_set"], 1)
                    dve.wait_ge(s["stats1"], b + 1)
                    for t in range(NT):
                        last = V.bn_aggr(mv1[:, t], bst1[:, t])
                    last.then_inc(s["mv1_done"], 1)

                def mean_shift(b):
                    dve.wait_ge(s["rstd1_done"], b + 1)
                    V.scalar_tensor_tensor(nmr1[:], mv1[:, :, 0], -1.0, rstd1[:], ALU.mult, ALU.mult).then_inc(s["nmr_done"], 1)

                def energy(b, t):
                    pass

                def softmax(b, t):
                    dve.wait_ge(s["energy_mm"], NT * b + t + 1)
                    V.tensor_reduce(nmax[:, t:t + 1], abank[t % 2][:], AX.X, ALU.max, negate=True).then_inc(s["max_done"], 1)

                def scale(b):
                    dve.wait_ge(s["exp_done"], NT * (b + 1))
                    V.reciprocal(rinv[:], rsum[:]).then_inc(s["rinv_done"], 1)
                    dve.wait_ge(s["rinv_done"], b + 1)
                    for t in range(NT):
                        V.tensor_scalar(prob[:, t], prob[:, t], rinv[:, t:t + 1], None, ALU.mult).then_inc(s["prob_done"], 1)

                def spread(r):
                    pass

                def residual(r):
                    dve.wait_ge(s["res_mm"], r + 1)
                    if r == 0:
                        dve.wait_ge(s["r_in"], 32)
                    if r >= 2:
                        dve.wait_ge(s["res_done"], r - 1)
                    if r < 2 * CLS:
                        c = slice(r % CLS * HID, (r % CLS + 1) * HID)
                        parts = r2g[:, c], r3g[:, c]
                    else:
                        m = r - 2 * CLS
                        if m % 4 == 0:
                            dve.wait_ge(s[f"rd{m // 4 % 3}_in"], 32 * (m // 12 + 1))
                        parts = (rd[m // 4 % 3][n][:, m % 4 * HID:(m % 4 + 1) * HID] for n in range(2))
                    for k, part in enumerate(parts):
                        V.tensor_tensor(prod2[:, r % 2, k], bank[2 * (r % 2) + k][:], part, ALU.mult).then_inc(s["res_mul"], 1)

                def prob_t(b, t):
                    pass

                def split_prob(b, t):
                    dve.wait_ge(s["ph_done"], NT * b + t + 1)
                    V.tensor_tensor(pl[:, t], abank[t % 2][:], ph[:, t].bitcast(f32), ALU.subtract).then_inc(s["pl_done"], 1)

                def split_x(b):
                    dve.wait_ge(s["xh_done"], b + 1)
                    V.tensor_tensor(xl[:], xT[:], xh[:].bitcast(f32), ALU.subtract).then_inc(s["xsplit_done"], 1)

                def tap_products(k):
                    pass

                def tap_sums(k):
                    c = chunk(k)
                    dve.wait_ge(s["tap_mul"], k + 1)
                    if k >= 2:
                        dve.wait_ge(s["stack_done"], k - 1)
                    V.tensor_reduce(c["sums"], c["prod"].rearrange("p (n t) -> p n t", t=4), AX.X, ALU.add).then_inc(s["tap_sum"], 1)

                def stack_parts(k):
                    c = chunk(k)
                    dve.wait_ge(s["stack_hi"], k + 1)
                    V.tensor_tensor(c["parts"][:, :, c["low"]].bitcast(f32r), c["val"], c["parts"][:, :, 0], ALU.subtract).then_inc(s["stack_done"], 1)

                def jump_inputs():
                    pass

                def jumps():
                    dve.wait_ge(s["jump_sums"], 4)
                    V.scalar_tensor_tensor(ja, jb, 2.0, ja, ALU.mult, ALU.add).then_inc(s["jump_d"], 1)
                    V.scalar_tensor_tensor(knots[:, 0], knots[:, 1], -4.0, knots[:, 0], ALU.mult, ALU.add).then_inc(s["jump_c"], 1)
                    dve.wait_ge(s["jump_k2"], 1)
                    dve.wait_ge(s["jump_c"], 1)
                    dve.wait_ge(s["jump_d"], 1)
                    V.scalar_tensor_tensor(jb, knots[:, 0], S2 / S3, knots[:, 2], ALU.mult, ALU.add).then_inc(s["jump_d"], 1)
                    for k in range(2):
                        dve.wait_ge(s["jump_hi"], k + 1)
                        V.tensor_tensor(jump[k][HALF:P], (ja, jb)[k][HALF:P], jump[k][HALF:P], ALU.subtract).then_inc(s["jump_split"], 1)

                def down_factors():
                    dve.wait_ge(s["du_hi"], 1)
                    V.tensor_tensor(d_u[:, :, 2], basis_f[:], d_u[:, :, 0].bitcast(f32), ALU.subtract).then_inc(s["du_done"], 1)

                def xm(b, t):
                    pass

                def add_xm(b, t):
                    dve.wait_ge(s["xm_scaled"], NT * b + t + 1)
                    V.tensor_tensor(x[:, t], x[:, t], xm_[:, t % 2], ALU.add).then_inc(s["x1_added"], 1)
                    dve.wait_ge(s["x1_added"], NT * b + t + 1)
                    V.bn_stats(bst2[:, t], x[:, t]).then_inc(s["stats2"], 1)
                    dve.wait_ge(s["consts_set"], 1)
                    dve.wait_ge(s["stats2"], NT * b + t + 1)
                    V.bn_aggr(mv2[:, t], bst2[:, t]).then_inc(s["mv2_done"], 1)
                    if t:
                        normalise(b, t - 1)
                    if t == NT - 1:
                        normalise(b, t)

                def cast_t(b, t):
                    dve.wait_ge(s["xn2t_copied"], NT * b + t + 1)
                    V.tensor_copy(xn2r[:, t], xn2T[:, t]).then_inc(s["xn2r_done"], 1)

                def norm_t(b, t):
                    pass

                def project(b):
                    dve.wait_ge(s["zg_hi"], b + 1)
                    dve.wait_ge(s["basis_in"], 3 * 16)
                    V.scalar_tensor_tensor(zg, zg.bitcast(f32), g_low[:], zgbank[0:G_K, :], ALU.mult, ALU.add).then_inc(s["zg_done"], 1)

                def gate_up(b, m):
                    pass

                def activate(b, m):
                    dve.wait_ge(s["silu_done"], MT * b + m + 1)
                    dve.wait_ge(s["u_mm"], MT * b + m + 1)
                    V.tensor_tensor(inter[:, m % 3], inter[:, m % 3], ubank[m % 2][:], ALU.mult).then_inc(s["mult_done"], 1)
                    dve.wait_ge(s["mult_done"], MT * b + m + 1)
                    V.tensor_copy(ih[:, m], inter[:, m % 3]).then_inc(s["ih_done"], 1)

                def down_basis(b, m):
                    pass

                def down_split(b, w):
                    dve.wait_ge(s["zd_hi"], WIN * b + w + 1)
                    V.scalar_tensor_tensor(zd[:, w], zd[:, w].bitcast(f32), d_low[:], zdbank[w][:], ALU.mult, ALU.add).then_inc(s["zd_done"], 1)

                def down(b, t, tiles):
                    pass

                def down_tail(b, t):
                    dve.wait_ge(s["out_mm"], NT * b + t + 1)
                    dve.wait_ge(s["x1_kept"], b + 1)
                    V.tensor_tensor(xres[:, t], xres[:, t], obank[t][:], ALU.add).then_inc(s["out_added"], 1)

            def normalise(b, t):
                dve.wait_ge(s["rstd2_done"], NT * b + t + 1)
                V.tensor_scalar(xn2[:, t], x[:, t], mv2[:, t, 0:1], rstd2[:, t:t + 1], ALU.subtract, ALU.mult).then_inc(s["xn2_done"], 1)

            xm_ = xm
            program(dve, Stages)

        @block.gpsimd
        def _(pool):
            G = nc.gpsimd

            class Stages:
                def constants():
                    pass

                def split_windows(a):
                    pass

                def qk(b):
                    pass

                def stats(b):
                    pool.wait_ge(s["consts_set"], 1)
                    pool.wait_ge(s["mv1_done"], b + 1)
                    G.tensor_tensor(ve1[:], mv1[:, :, 1], eps[:], ALU.add).then_inc(s["ve1_done"], 1)
                    pool.wait_ge(s["ve1_done"], b + 1)
                    G.tensor_tensor(rstd1[:], ve1[:], neghalf[:], ALU.pow).then_inc(s["rstd1_done"], 1)

                def energy(b, t):
                    pass

                def softmax(b, t):
                    pass

                def mean_shift(b):
                    pass

                def scale(b):
                    pass

                def spread(r):
                    pass

                def residual(r):
                    pool.wait_ge(s["res_mul"], 2 * r + 2)
                    if r < 2 * CLS:
                        dst = gu_r[r // CLS][:, r % CLS]
                    else:
                        if r == 2 * CLS:
                            pool.wait_ge(s["tap_mul"], 8)
                        if r == 2 * CLS + 8:
                            pool.wait_ge(s["tap_mul"], CHUNKS)
                        if r == 2 * CLS + MT - 2:
                            pool.wait_ge(s["du_done"], 1)
                        dst = d_r[:, r - 2 * CLS]
                    G.tensor_tensor(dst, prod2[:, r % 2, 0], prod2[:, r % 2, 1], ALU.add).then_inc(s["res_done"], 1)

                def prob_t(b, t):
                    pass

                def split_prob(b, t):
                    pass

                def split_x(b):
                    pass

                def tap_products(k):
                    c = chunk(k)
                    if k in (0, 4, 8):
                        need, count = {0: ("node_in", 32), 4: ("upnode_in", 16), 8: ("dnode_in", 32)}[k]
                        pool.wait_ge(s[need], count)
                    if k >= 2:
                        pool.wait_ge(s["tap_sum"], k - 1)
                    G.tensor_tensor(c["prod"].rearrange("p (n v t) -> p n v t", v=2, t=4), c["coef"], c["points"], ALU.mult).then_inc(s["tap_mul"], 1)

                def tap_sums(k):
                    pass

                def stack_parts(k):
                    pass

                def jump_inputs():
                    pool.wait_ge(s["knot_in"], 32)
                    pool.wait_ge(s["win_split"], CLS)
                    G.tensor_tensor(ja, knots[:, 0], knots[:, 4], ALU.subtract).then_inc(s["jump_sums"], 1)
                    G.tensor_tensor(jb, knots[:, 3], knots[:, 1], ALU.subtract).then_inc(s["jump_sums"], 1)
                    pool.wait_ge(s["jump_sums"], 2)
                    G.tensor_tensor(knots[:, 0], knots[:, 0], knots[:, 4], ALU.add).then_inc(s["jump_sums"], 1)
                    G.tensor_tensor(knots[:, 1], knots[:, 1], knots[:, 3], ALU.add).then_inc(s["jump_sums"], 1)

                def jumps():
                    pass

                def down_factors():
                    pass

                def xm(b, t):
                    pass

                def add_xm(b, t):
                    pool.wait_ge(s["mv2_done"], NT * b + t + 1)
                    G.tensor_tensor(ve2[:, t:t + 1], mv2[:, t, 1:2], eps[:, t:t + 1], ALU.add).then_inc(s["ve2_done"], 1)
                    pool.wait_ge(s["ve2_done"], NT * b + t + 1)
                    G.tensor_tensor(rstd2[:, t:t + 1], ve2[:, t:t + 1], neghalf[:, t:t + 1], ALU.pow).then_inc(s["rstd2_done"], 1)

                def cast_t(b, t):
                    pass

                def norm_t(b, t):
                    pass

                def project(b):
                    pool.wait_ge(s["res_done"], 2 * CLS + MT)
                    pool.wait_ge(s["x1_added"], NT * (b + 1))
                    pool.wait_ge(s["out_stored"], 16 * NT * b + 1)
                    G.tensor_tensor(xres[:], x[:], ones[:].broadcast_to([P, NT, HID]), ALU.mult).then_inc(s["x1_kept"], 1)

                def gate_up(b, m):
                    pass

                def activate(b, m):
                    pool.wait_ge(s["ih_done"], MT * b + m + 1)
                    if m >= 2:
                        pool.wait_ge(s["zd_mm"], MT * b + m - 1)
                    G.tensor_tensor(il[:, m % 2], inter[:, m % 3], ih[:, m].bitcast(f32), ALU.subtract).then_inc(s["il_done"], 1)

                def down_basis(b, m):
                    pass

                def down_split(b, w):
                    pass

                def down(b, t, tiles):
                    pass

                def down_tail(b, t):
                    pass

            program(pool, Stages)

        @block.tensor
        def _(pe):
            mm = nc.tensor.matmul

            class Stages:
                def constants():
                    pe.wait_ge(s["wqk_in"], 2 * 16)

                def split_windows(a):
                    pass

                def qk(b):
                    pe.wait_ge(s["ctx_in"], 16 * (b + 1))
                    pe.wait_ge(s["xn2t_copied"], NT * b)
                    for n in range(2):
                        for c in range(CTX // P):
                            last = mm(abank[n][:], wqk[:, n, c], ctxT[:, c], start=c == 0, stop=c == CTX // P - 1)
                        last.then_inc(s["qk_mm"], 1)

                def stats(b):
                    pass

                def energy(b, t):
                    if t == 0:
                        pe.wait_ge(s["qk_done"], 2 * b + 2)
                    if t >= 2:
                        pe.wait_ge(s["exp_done"], NT * b + t - 1)
                    mm(abank[t % 2][:], qk_[:, 0, t * P:(t + 1) * P], qk_[:, 1], start=True, stop=True).then_inc(s["energy_mm"], 1)

                def softmax(b, t):
                    pass

                def mean_shift(b):
                    pass

                def scale(b):
                    pass

                def residual(r):
                    pass

                def spread(r):
                    if r >= 2:
                        pe.wait_ge(s["res_mul"], 2 * (r - 1))
                    if r < CLS:
                        pe.wait_ge(s["win_split"], r + 1)
                    if r == 2 * CLS:
                        pe.wait_ge(s["jump_split"], 2)
                    for k in range(2):
                        dst = bank[2 * (r % 2) + k][:]
                        if r < 2 * CLS:
                            p, c = HALF * (r // CLS), slice(r % CLS * HID, (r % CLS + 1) * HID)
                            last = mm(dst, pick[p:p + HALF, r % CLS, k], win_hl[p:p + HALF, c], start=True, stop=True)
                        else:
                            last = mm(dst, spread_[:, r - 2 * CLS], jump[k], start=True, stop=True)
                    last.then_inc(s["res_mm"], 1)

                def prob_t(b, t):
                    if t == 0:
                        pe.wait_ge(s["ident_in"], 16)
                        pe.wait_ge(s["prob_done"], NT * (b + 1))
                    if t >= 2:
                        pe.wait_ge(s["pl_done"], NT * b + t - 1)
                    for m in range(NT):
                        last = nc.tensor.transpose(abank[t % 2][:, m * P:(m + 1) * P], prob[:, m, t * P:(t + 1) * P], ident[:])
                    last.then_inc(s["pT_mm"], 1)

                def split_prob(b, t):
                    pass

                def split_x(b):
                    pass

                def tap_products(k):
                    pass

                def tap_sums(k):
                    pass

                def stack_parts(k):
                    c = chunk(k)
                    if k == 0:
                        pe.wait_ge(s["ident_in"], 16)
                    pe.wait_ge(s["stack_done"], k + 1)
                    if k >= 2:
                        pe.wait_ge(s["stack_out"], k - 1)
                    for n in range(4):
                        last = nc.tensor.transpose(bank[4 + k % 2][0:c["width"], n * P:(n + 1) * P],
                                                   c["stack"][:, n * c["width"]:(n + 1) * c["width"]], ident[:])
                    last.then_inc(s["stack_mm"], 1)

                def jump_inputs():
                    pass

                def jumps():
                    pass

                def down_factors():
                    pass

                def xm(b, t):
                    if t == 0:
                        pe.wait_ge(s["xsplit_done"], b + 1)
                        pe.wait_ge(s["pl_done"], NT * (b + 1))
                    if t >= 2:
                        pe.wait_ge(s["xm_scaled"], NT * b + t - 1)
                    c = slice(t * P, (t + 1) * P)
                    for n in range(NT):
                        mm(abank[t % 2][:], xh[:, n, c], ph[:, n], start=n == 0, stop=False)
                        mm(abank[t % 2][:], xh[:, n, c], pl[:, n], start=False, stop=False)
                        last = mm(abank[t % 2][:], xl[:, n, c], ph[:, n], start=False, stop=n == NT - 1)
                    last.then_inc(s["xm_mm"], 1)

                def add_xm(b, t):
                    pass

                def norm_t(b, t):
                    if t == 0:
                        pe.wait_ge(s["xn2_done"], NT * (b + 1))
                        pe.wait_ge(s["xm_scaled"], NT * (b + 1))
                    if t >= 2:
                        pe.wait_ge(s["xn2t_copied"], NT * b + t - 1)
                    for l in range(NT):
                        last = nc.tensor.transpose(abank[t % 2][:, l * P:(l + 1) * P], xn2[:, l, t * P:(t + 1) * P], ident[:])
                    last.then_inc(s["xn2T_mm"], 1)

                def cast_t(b, t):
                    pass

                def project(b):
                    pe.wait_ge(s["xn2t_copied"], NT * (b + 1))
                    pe.wait_ge(s["stack_out"], CHUNKS)
                    pe.wait_ge(s["basis_in"], 3 * 16)
                    for a in range(CLS):
                        last = mm(zgbank[0:G_K, :], g_basis[:, a], xn2T[:, a], start=a == 0, stop=a == CLS - 1)
                    last.then_inc(s["zg_mm"], 1)

                def gate_up(b, m):
                    w, a = m // CLS, m % CLS
                    if m == 0:
                        pe.wait_ge(s["zg_done"], b + 1)
                        pe.wait_ge(s["xn2r_done"], NT * (b + 1))
                        pe.wait_ge(s["res_done"], 2 * CLS + MT)
                    for n, (dst, read) in enumerate(((gbank, "silu_done"), (ubank, "mult_done"))):
                        if m >= 2:
                            pe.wait_ge(s[read], MT * b + m - 1)
                        mm(dst[m % 2][:], gu_r[n][:, a, w * P:(w + 1) * P], xn2r[:, a], start=True, stop=False)
                    for n, (dst, done) in enumerate(((gbank, "g_mm"), (ubank, "u_mm"))):
                        mm(dst[m % 2][:], gu_v[n][:, m], zg, start=False, stop=True).then_inc(s[done], 1)

                def activate(b, m):
                    pass

                def down_basis(b, m):
                    w, a = m // CLS, m % CLS
                    if a == 0 and w >= 2:
                        pe.wait_ge(s["zd_done"], WIN * b + w - 1)
                    if m == 0:
                        pe.wait_ge(s["du_done"], 1)
                    pe.wait_ge(s["il_done"], MT * b + m + 1)
                    u = d_u[:, m].rearrange("p k f -> p (k f)")
                    mm(zdbank[w][:], u, ih[:, m], start=a == 0, stop=False)
                    mm(zdbank[w][:], u, il[:, m % 2], start=False, stop=a == CLS - 1).then_inc(s["zd_mm"], 1)

                def down_split(b, w):
                    pass

                def down(b, t, tiles):
                    if t == 0:
                        if tiles[0] == 0:
                            pe.wait_ge(s["silu_done"], MT * b + MT - 1)
                        pe.wait_ge(s["ih_done"], MT * b + tiles[-1] + 1)
                    if t == 1:
                        pe.wait_ge(s["mult_done"], MT * (b + 1))
                    for m in tiles:
                        mm(obank[t][:], ih[:, m, t * P:(t + 1) * P], d_r[:, m], start=m == 0, stop=False)

                def down_tail(b, t):
                    if t == 0:
                        pe.wait_ge(s["zd_done"], WIN * (b + 1))
                    for w in range(WIN):
                        last = mm(obank[t][:], zd[:, w, t * P:(t + 1) * P], d_v[:, w], start=False, stop=w == WIN - 1)
                    last.then_inc(s["out_mm"], 1)

            qk_, spread_ = qk, spread
            program(pe, Stages)


def kernel(x, ctx_1024, L0_xattn_Wq, L0_xattn_bq, L0_xattn_Wk, L0_xattn_bk, L0_ffn_gate_cp, L0_ffn_up_cp, L0_ffn_down_cp):
    import concourse.bacc as bacc
    from concourse.bass_utils import run_bass_kernel_spmd

    c, at, hidden, _ = constants()
    x, ctx_1024, wq, bq, wk, bk, gate, up, down = (np.asarray(a) for a in (
        x, ctx_1024, L0_xattn_Wq, L0_xattn_bq, L0_xattn_Wk, L0_xattn_bk, L0_ffn_gate_cp, L0_ffn_up_cp, L0_ffn_down_cp))
    x, context = x[:, :, hidden], ctx_1024[:, hidden]

    def tiled(a):
        return a.reshape(*a.shape[:-2], -1, P, a.shape[-1]).swapaxes(-3, -2)

    arrays = dict(
        c, x=tiled(x), xT=tiled(x.swapaxes(1, 2)), ctxT=tiled(context.swapaxes(1, 2)),
        wqT=tiled(wq.T), wkT=tiled(wk.T), bq=bq.reshape(DK, 1), bk=bk.reshape(DK, 1),
        g_node=gate[at["g_node"]].reshape(P, -1), u_node=up[at["g_node"]].reshape(P, -1),
        g_win=gate[at["g_win"]], u_win=up[at["g_win"]],
        d_node=down[at["d_node"]].reshape(P, -1), d_knot=down[at["d_knot"]].reshape(P, -1))
    arrays = {f"in_{k}": np.ascontiguousarray(v) for k, v in arrays.items()}
    nc = bacc.Bacc("TRN2", target_bir_lowering=False, num_devices=1)
    d = {k[3:]: nc.dram_tensor(k, v.shape, mybir.dt.from_np(v.dtype), kind="ExternalInput").ap() for k, v in arrays.items()}
    out = nc.dram_tensor("out", (B, NT, P, HID), mybir.dt.float32, kind="ExternalOutput").ap()
    xattn_spline_ffn_kernel(nc, d, out)
    got = run_bass_kernel_spmd(nc, [arrays], core_ids=[0]).results[0]["out"]
    back = np.argsort(hidden)
    return np.ascontiguousarray(got.reshape(B, TOK, HID)[:, :, back])
```
